# Optimizing a Trainium2 kernel written in Bass

```python
import numpy as np
import jax
import jax.numpy as jnp

def _softmax(x, axis=-1):
    return jax.nn.softmax(x, axis=axis)

def _gelu(x):
    return jax.nn.gelu(x, approximate=True)

def _silu(x):
    return jax.nn.silu(x)

def _sigmoid(x):
    return jax.nn.sigmoid(x)

def _layernorm(x, axis=-1, eps=1e-05):
    m = jnp.mean(x, axis=axis, keepdims=True)
    v = jnp.var(x, axis=axis, keepdims=True)
    return (x - m) / jnp.sqrt(v + eps)

def _scatter_add(tgt, idx, src, axis=0):
    return tgt.at[idx].add(src)

def _segment_sum(src, seg, n):
    return jax.ops.segment_sum(src, seg, n)
kernel_name = 'mk_seq_postln_d1_jaxref_r4_f3922a'

def setup_inputs(seed: int=0):
    np.random.seed(seed)
    _w = jnp.asarray

    def _L0_attn_setup():
        import jax, jax.numpy as jnp
        import numpy as np
        B, SEQ, EMBED, HEADS = (1, 1024, 1024, 16)
        HEAD_DIM = EMBED // HEADS
        ROT = 64
        MASKED_BIAS = -1000000000.0

        def _rotate_every_two(x):
            x1 = x[..., ::2]
            x2 = x[..., 1::2]
            return jnp.stack((-x2, x1), axis=-1).reshape(x.shape)

        def _apply_rope(x, sin, cos):
            sin = jnp.repeat(sin, 2, axis=-1)[None, :, None, :]
            cos = jnp.repeat(cos, 2, axis=-1)[None, :, None, :]
            return x * cos + _rotate_every_two(x) * sin
        key = jax.random.key(seed)
        ks = jax.random.split(key, 5)
        s = 0.02
        return {'hidden_states': jax.random.normal(ks[0], (B, SEQ, EMBED), jnp.float32), 'w_q': jax.random.normal(ks[1], (EMBED, EMBED), jnp.float32) * s, 'w_k': jax.random.normal(ks[2], (EMBED, EMBED), jnp.float32) * s, 'w_v': jax.random.normal(ks[3], (EMBED, EMBED), jnp.float32) * s, 'w_out': jax.random.normal(ks[4], (EMBED, EMBED), jnp.float32) * s}
    _L0_attn_in = _L0_attn_setup()

    def _L0_ffn_setup():
        import jax, jax.numpy as jnp
        import numpy as np
        key = jax.random.key(seed)
        k1, k2, k3 = jax.random.split(key, 3)
        B, S, D_in, D_out = (4, 512, 1024, 1024)
        x = jax.random.normal(k1, (B, S, D_in), dtype=jnp.float32)
        weight = jax.random.randint(k2, (D_out, D_in), -32, 32, dtype=jnp.int32).astype(jnp.int8)
        scales = (jax.random.uniform(k3, (D_out,), dtype=jnp.float32) * 0.002 + 0.0005).astype(jnp.float16)
        return {'x': x, 'weight': weight, 'scales': scales}
    _L0_ffn_in = _L0_ffn_setup()
    _d = {'L0_attn_hidden_states': _L0_attn_in['hidden_states'], 'L0_attn_w_q': _L0_attn_in['w_q'], 'L0_attn_w_k': _L0_attn_in['w_k'], 'L0_attn_w_v': _L0_attn_in['w_v'], 'L0_attn_w_out': _L0_attn_in['w_out'], 'L0_ffn_weight': _L0_ffn_in['weight'], 'L0_ffn_scales': _L0_ffn_in['scales']}
    _x0 = _d['L0_attn_hidden_states']
    _d['L0_attn_hidden_states'] = jax.random.normal(jax.random.fold_in(jax.random.key(seed), 1), (4, 512, 1024), dtype=_x0.dtype)
    del _x0
    return _d

def reference(L0_attn_hidden_states, L0_attn_w_q, L0_attn_w_k, L0_attn_w_v, L0_attn_w_out, L0_ffn_weight, L0_ffn_scales):

    def _L0_attn_ref(hidden_states, w_q, w_k, w_v, w_out):
        import jax, jax.numpy as jnp
        import numpy as np
        B, SEQ, EMBED, HEADS = (1, 1024, 1024, 16)
        HEAD_DIM = EMBED // HEADS
        ROT = 64
        MASKED_BIAS = -1000000000.0

        def _rotate_every_two(x):
            x1 = x[..., ::2]
            x2 = x[..., 1::2]
            return jnp.stack((-x2, x1), axis=-1).reshape(x.shape)

        def _apply_rope(x, sin, cos):
            sin = jnp.repeat(sin, 2, axis=-1)[None, :, None, :]
            cos = jnp.repeat(cos, 2, axis=-1)[None, :, None, :]
            return x * cos + _rotate_every_two(x) * sin
        Bt, S, E = hidden_states.shape
        q = (hidden_states @ w_q.T).reshape(Bt, S, HEADS, HEAD_DIM)
        k = (hidden_states @ w_k.T).reshape(Bt, S, HEADS, HEAD_DIM)
        v = (hidden_states @ w_v.T).reshape(Bt, S, HEADS, HEAD_DIM)
        inv_freq = 1.0 / 10000.0 ** (jnp.arange(0, ROT, 2, dtype=jnp.float32) / ROT)
        sinusoid = jnp.arange(S, dtype=jnp.float32)[:, None] * inv_freq[None, :]
        sin, cos = (jnp.sin(sinusoid), jnp.cos(sinusoid))
        q = jnp.concatenate([_apply_rope(q[..., :ROT], sin, cos), q[..., ROT:]], axis=-1)
        k = jnp.concatenate([_apply_rope(k[..., :ROT], sin, cos), k[..., ROT:]], axis=-1)
        q = q.transpose(0, 2, 1, 3).astype(jnp.float32)
        k = k.transpose(0, 2, 1, 3).astype(jnp.float32)
        v = v.transpose(0, 2, 1, 3)
        scores = jnp.einsum('bhqd,bhkd->bhqk', q, k)
        causal = jnp.tril(jnp.ones((S, S), dtype=bool))[None, None]
        scores = jnp.where(causal, scores, MASKED_BIAS)
        scores = scores / jnp.sqrt(jnp.float32(HEAD_DIM))
        attn = jax.nn.softmax(scores, axis=-1).astype(v.dtype)
        out = jnp.einsum('bhqk,bhkd->bhqd', attn, v)
        out = out.transpose(0, 2, 1, 3).reshape(Bt, S, E)
        return out @ w_out.T

    def _L0_ffn_ref(x, weight, scales):
        import jax, jax.numpy as jnp
        import numpy as np
        w_dequant = weight.astype(jnp.float32) * scales.astype(jnp.float32)[:, None]
        return jnp.einsum('bsi,oi->bso', x, w_dequant)
    x = L0_attn_hidden_states
    x = _layernorm(x + _L0_attn_ref(x, L0_attn_w_q, L0_attn_w_k, L0_attn_w_v, L0_attn_w_out), axis=-1)
    x = _layernorm(x + _L0_ffn_ref(x, L0_ffn_weight, L0_ffn_scales), axis=-1)
    return x

_drawn_inputs = setup_inputs


def setup_inputs(seed=0):
    import zlib

    import numpy as np

    out = dict(_drawn_inputs(seed))
    spreads = {}
    factors = {}
    for name, (base, spread) in spreads.items():
        noise = np.random.default_rng([zlib.crc32(name.encode()), seed]).standard_normal(out[name].shape)
        drawn = base * np.exp(spread * noise) if base else spread * noise
        out[name] = jnp.asarray(drawn.astype(out[name].dtype))
    for name, factor in factors.items():
        out[name] = (out[name] * factor).astype(out[name].dtype)
    return out
```

```python
from contextlib import ExitStack

import concourse.bass as bass
from concourse import mybir

F32 = mybir.dt.float32
F32R = mybir.dt.float32r
F16 = mybir.dt.float16
I8 = mybir.dt.int8
I32 = mybir.dt.int32
ACT = mybir.ActivationFunctionType
ALU = mybir.AluOpType

P = 128
BATCHES, SEQ, EMBED = 4, 512, 1024
HEADS, HEAD_DIM = 16, 64
GROUPS = 4
GROUP_HEADS = HEADS // GROUPS
TOK_TILES = SEQ // P
E_TILES = EMBED // P
TASKS = TOK_TILES * GROUP_HEADS
UNIT = 1024
G_UNITS, WO_UNITS, W8_UNITS, X_UNITS = 6, 8, 8, 4
HALF = EMBED // 2
SCALE = float(HEAD_DIM) ** -0.5
MASKED = -1.0e30
EPS = 1e-05
QKU, VU = 4, 2
STEPS = TASKS + 2


def layer_program(nc, x_units, x_rows, w_units, w8_units, scales, cos_table, sin_table, out):
    ctx = ExitStack()
    with ctx:
        def sb(name, shape, dt=F32):
            return ctx.enter_context(nc.sbuf_tensor(name, shape, dt))

        def pb(name):
            return ctx.enter_context(nc.psum_tensor(name, [P, 512], F32))

        def sem(name):
            return ctx.enter_context(nc.semaphore(name))

        x_raw = [sb(f"x_raw{i}", [P, UNIT]) for i in range(2)]
        w_raw = [sb(f"w_raw{i}", [P, UNIT]) for i in range(2)]
        w_hi = [sb(f"w_hi{i}", [P, UNIT], F32R) for i in range(4)]
        w_lo = [sb(f"w_lo{i}", [P, UNIT], F32R) for i in range(4)]
        x_hi = sb("x_hi", [P, E_TILES, SEQ], F32R)
        x_lo = sb("x_lo", [P, E_TILES, SEQ], F32R)
        ot_hi = sb("ot_hi", [P, TOK_TILES, E_TILES, P], F32R)
        ot_lo = sb("ot_lo", [P, TOK_TILES, E_TILES, P], F32R)
        w8_raw = sb("w8_raw", [P, W8_UNITS * UNIT // 4], I32)
        w8 = w8_raw[:, :].bitcast(I8).rearrange("p (u c) -> p u c", u=W8_UNITS)
        y = [sb(f"y{t}", [P, EMBED]) for t in range(TOK_TILES)]
        qk_hi = sb("qk_hi", [P, QKU, SEQ], F32R)
        qk_lo = sb("qk_lo", [P, QKU, SEQ], F32R)
        qk_raw = [sb(f"qk_raw{u}", [P, SEQ]) for u in range(QKU)]
        qk_swap = [sb(f"qk_swap{i}", [P, SEQ]) for i in range(2)]
        cos_sb = sb("cos_sb", [P, SEQ])
        sin_sb = sb("sin_sb", [P, SEQ])
        v_sb = sb("v_sb", [P, TOK_TILES, GROUP_HEADS, 2 * HEAD_DIM], F32R)
        prob = [sb(f"prob{i}", [P, SEQ]) for i in range(2)]
        pt_hi = [sb(f"pt_hi{i}", [P, SEQ], F32R) for i in range(2)]
        pt_lo = [sb(f"pt_lo{i}", [P, SEQ], F32R) for i in range(2)]
        o_lo = sb("o_lo", [P, GROUP_HEADS, HEAD_DIM])
        o_sum = sb("o_sum", [P, GROUP_HEADS, HEAD_DIM])
        o_norm = sb("o_norm", [P, GROUP_HEADS, HEAD_DIM])
        mask = sb("mask", [P, SEQ])
        ident = sb("ident", [P, P])
        scale_sb = sb("scale_sb", [P, EMBED])
        scale_raw = sb("scale_raw", [P, EMBED], F16)
        z_mul_sb = [sb(f"z_mul_sb{h}", [P, HALF]) for h in range(2)]
        neg_max = sb("neg_max", [P, 2])
        row_sum = sb("row_sum", [P, 2, GROUP_HEADS])
        row_rec = sb("row_rec", [P, GROUP_HEADS])
        stats = sb("stats", [P, TOK_TILES, 12])
        mean_var = sb("mean_var", [P, TOK_TILES, 2])
        var_eps = sb("var_eps", [P, TOK_TILES])
        rstd = sb("rstd", [P, TOK_TILES])
        minus_half = sb("minus_half", [P, 1])
        turn = sb("turn", [P, 2 + TOK_TILES])

        u_ps = [pb("u_ps0"), pb("u_ps1")]
        s_ps = [pb("s_ps0"), pb("s_ps1")]
        t_ps = [pb("t_ps0"), pb("t_ps1")]
        pv_ps = pb("pv_ps")
        ott_ps = pb("ott_ps")

        w_loaded = [sem(f"w_loaded{i}") for i in range(2)]
        x_loaded = [sem(f"x_loaded{i}") for i in range(2)]
        y_loaded = [sem(f"y_loaded{t}") for t in range(TOK_TILES)]
        stored = [sem(f"stored{t}") for t in range(TOK_TILES)]
        swapped = [sem(f"swapped{i}") for i in range(2)]
        tables_loaded = sem("tables_loaded")
        w8_loaded = sem("w8_loaded")
        consts_ready = sem("consts_ready")
        consts_step = sem("consts_step")
        scale_ready = sem("scale_ready")
        w_hi_ready, w_ready = sem("w_hi_ready"), sem("w_ready")
        x_hi_ready, x_ready = sem("x_hi_ready"), sem("x_ready")
        qk_done, v_done = sem("qk_done"), sem("v_done")
        qk_evacuated = sem("qk_evacuated")
        sin_mul, cos_mul, roped = sem("sin_mul"), sem("cos_mul"), sem("roped")
        qk_hi_ready, qk_ready = sem("qk_hi_ready"), sem("qk_ready")
        v_hi_ready, v_ready = sem("v_hi_ready"), sem("v_ready")
        s_done, max_done, exp_done = sem("s_done"), sem("max_done"), sem("exp_done")
        t_done, pt_hi_ready, pt_ready = sem("t_done"), sem("pt_hi_ready"), sem("pt_ready")
        pv_done, o_lo_ready, rec_done = sem("pv_done"), sem("o_lo_ready"), sem("rec_done")
        o_sum_done, o_ready, ott_done = sem("o_sum_done"), sem("o_ready"), sem("ott_done")
        ot_hi_ready, ot_ready = sem("ot_hi_ready"), sem("ot_ready")
        wo_slot_free, op_done, op_added = sem("wo_slot_free"), sem("op_done"), sem("op_added")
        stats_done, mv_done, ve_done = sem("stats_done"), sem("mv_done"), sem("ve_done")
        rstd_ready, x1_done = sem("rstd_ready"), sem("x1_done")
        x1tt_done, x1t_hi_ready, x1t_ready = sem("x1tt_done"), sem("x1t_hi_ready"), sem("x1t_ready")
        w8_ready, w8_free, ffn_done = sem("w8_ready"), sem("w8_free"), sem("ffn_done")
        z_mul, z_added, z_done = sem("z_mul"), sem("z_added"), sem("z_done")

        block = ctx.enter_context(nc.Block())

        def f32(ap):
            return ap.bitcast(F32)

        def task(tau):
            i = TOK_TILES - 1 - tau // GROUP_HEADS
            return i, tau % GROUP_HEADS, P * (i + 1)

        def g_pos(m, tails):
            return m * G_UNITS + tails * WO_UNITS

        def wo_pos(groups, b):
            return groups * G_UNITS + b * WO_UNITS

        G_SLOT = [0, 1, 0, 1, 2, 3]
        SPLIT_STEP = {2: 3, 3: 6, 4: 8, 5: 9}
        AHEAD_STEP = {0: 10, 1: 12}

        def program(body, tail, prologue, eng):
            prologue()
            with eng.Fori(0, BATCHES - 1) as b:
                with eng.Fori(0, GROUPS - 1) as g:
                    body(b, g, ahead="group")
                body(b, GROUPS - 1, ahead="wo", new_x=True)
                tail(b, b * GROUPS + (GROUPS + 1))
            last = BATCHES - 1
            with eng.Fori(0, GROUPS - 2) as g:
                body(last, g, ahead="group")
            body(last, GROUPS - 2, ahead="wo")
            body(last, GROUPS - 1, ahead=None, fill=False)
            tail(last, BATCHES * GROUPS)

        @block.sync
        def _(sp):
            def load_w(row, pos, unit, wait=True):
                i = unit % 2
                if wait:
                    sp.wait_ge(w_ready, pos - 1)
                sp.wait_ge(consts_ready, 1)
                sp.dma_start(w_raw[i][:, :], w_units[row, :, :]).then_inc(w_loaded[i], 16)

            def load_x(b, x, wait=True):
                if wait:
                    sp.wait_ge(x_ready, b * X_UNITS + (x - 1))
                    sp.wait_ge(consts_ready, 1)
                sp.dma_start(x_raw[x % 2][:, :], x_units[b * X_UNITS + x, :, :]).then_inc(x_loaded[x % 2], 16)

            def load_rows(b, t):
                sp.dma_start(y[t][:, :], x_rows[b * TOK_TILES + t, :, :]).then_inc(y_loaded[t], 16)

            def prologue():
                g0 = (GROUPS - 1) * G_UNITS
                sp.dma_start(w_raw[0][:, :], w_units[g0, :, :]).then_inc(w_loaded[0], 16)
                for x in range(X_UNITS):
                    load_x(0, x, wait=x >= 2)
                sp.dma_start(w_raw[1][:, :], w_units[g0 + 1, :, :]).then_inc(w_loaded[1], 16)
                sp.dma_start(cos_sb[:, :], cos_table).then_inc(tables_loaded, 16)
                sp.dma_start(sin_sb[:, :], sin_table).then_inc(tables_loaded, 16)
                sp.dma_start(scale_raw[:, :], scales.partition_broadcast(P)).then_inc(tables_loaded, 16)
                for k in range(2, G_UNITS):
                    load_w(g0 + k, k, k)
                for k in range(2):
                    load_w(k, G_UNITS + k, k)
                sp.dma_start(w8_raw[:, :], w8_units).then_inc(w8_loaded, 16)
                for t in range(TOK_TILES):
                    load_rows(0, t)

            def body(b, g, ahead, fill=True, new_x=False):
                n = b * GROUPS + g
                m, tails = n + 1, b
                if new_x:
                    for x in range(X_UNITS):
                        load_x(b + 1, x)
                if fill:
                    for k in range(2, G_UNITS):
                        load_w(g * G_UNITS + k, g_pos(m, tails) + k, k)
                for k in range(2):
                    if ahead == "group":
                        load_w((g + 1) * G_UNITS + k, g_pos(m + 1, tails) + k, k)
                    elif ahead == "wo":
                        load_w(GROUPS * G_UNITS + k, g_pos(m + 1, tails) + k, k)

            def tail(b, groups):
                for w in range(2, WO_UNITS):
                    load_w(GROUPS * G_UNITS + w, wo_pos(groups, b) + w, w)
                if groups is not BATCHES * GROUPS:
                    for k in range(2):
                        load_w(k, wo_pos(groups, b) + WO_UNITS + k, k)
                for t in range(TOK_TILES):
                    sp.wait_ge(z_done, b * TOK_TILES + (t + 1))
                    sp.wait_ge(consts_ready, 1)
                    sp.dma_start(out[b * TOK_TILES + t, :, :], y[t][:, :]).then_inc(stored[t], 16)
                if groups is not BATCHES * GROUPS:
                    for t in range(TOK_TILES):
                        sp.wait_ge(stored[t], b * 16 + 16)
                        sp.wait_ge(consts_ready, 1)
                        load_rows(b + 1, t)

            program(body, tail, prologue, sp)
            for t in range(TOK_TILES):
                sp.wait_ge(stored[t], BATCHES * 16)

        @block.gpsimd
        def _(pool):
            def split_lo(pos, loads, unit, slot):
                pool.wait_ge(w_hi_ready, pos + 1)
                nc.gpsimd.tensor_tensor(w_lo[slot][:, :], w_raw[unit % 2][:, :], f32(w_hi[slot][:, :]),
                                        ALU.subtract).then_inc(w_ready, 1)

            def rotate_sin(m, u):
                pool.wait_ge(swapped[u % 2], (m * 2 + u // 2 + 1) * 64)
                if isinstance(m, int) and m == 0 and u == 0:
                    pool.wait_ge(tables_loaded, 48)
                nc.gpsimd.tensor_tensor(qk_swap[u % 2][:, :], qk_swap[u % 2][:, :], sin_sb[:, :],
                                        ALU.mult).then_inc(sin_mul, 1)

            def group(m, tails, ahead_m, ahead):
                for s in range(STEPS + 2):
                    for k, at in SPLIT_STEP.items():
                        if at == s and m is not None:
                            split_lo(g_pos(m, tails) + k, None, k, G_SLOT[k])
                    for k, at in AHEAD_STEP.items():
                        if at == s and ahead:
                            split_lo(g_pos(ahead_m, tails) + k, None, k, k)
                    if s >= 5 and (s - 5) % 3 == 0 and (s - 5) // 3 < QKU and m is not None:
                        rotate_sin(m, (s - 5) // 3)

            def prologue():
                nc.gpsimd.memset(mask[:, :], 0.0).then_inc(consts_step, 1)
                nc.gpsimd.memset(ident[:, :], 0.0).then_inc(consts_step, 1)
                nc.gpsimd.memset(minus_half[:, :], -0.5).then_inc(consts_step, 1)
                pool.wait_ge(consts_step, 3)
                nc.gpsimd.affine_select(out=mask[:, SEQ - P:SEQ], in_=mask[:, SEQ - P:SEQ],
                                        compare_op=ALU.is_ge, fill=MASKED, base=0, pattern=[[-1, P]],
                                        channel_multiplier=1).then_inc(consts_step, 1)
                nc.gpsimd.affine_select(out=ident[:, :], in_=ident[:, :], compare_op=ALU.not_equal, fill=1.0,
                                        base=0, pattern=[[-1, P]], channel_multiplier=1).then_inc(consts_step, 1)
                pool.wait_ge(consts_step, 5)
                nc.gpsimd.memset(minus_half[:, :], -0.5).then_inc(consts_ready, 1)
                for k in range(2):
                    split_lo(k, None, k, k)
                group(0, 0, 1, "group")

            def body(b, g, ahead, fill=True, new_x=False):
                n = b * GROUPS + g
                group(n + 1 if fill else None, b, n + 2, ahead)

            def tail(b, groups):
                for w in range(2, WO_UNITS):
                    split_lo(wo_pos(groups, b) + w, None, w, w % 4)

                def rsqrt(which, t):
                    pool.wait_ge(ve_done, b * 8 + (4 * which + t + 1))
                    nc.gpsimd.tensor_tensor(rstd[:, t:t + 1], var_eps[:, t:t + 1], minus_half[:, :],
                                            ALU.pow).then_inc(rstd_ready, 1)
                for t in range(TOK_TILES):
                    rsqrt(0, t)
                for t in range(TOK_TILES - 1):
                    rsqrt(1, t)
                if groups is not BATCHES * GROUPS:
                    for k in range(2):
                        pool.wait_ge(w8_free, b * 3 + (k + 1))
                        split_lo(wo_pos(groups, b) + WO_UNITS + k, None, k, k)
                rsqrt(1, TOK_TILES - 1)

            program(body, tail, prologue, pool)

        @block.scalar
        def _(act):
            def copy(dst, src):
                return nc.scalar.activation(dst, src, ACT.Copy)

            def split_hi(loads, unit, slot):
                act.wait_ge(w_loaded[unit % 2], (loads + 1) * 16)
                copy(w_hi[slot][:, :], w_raw[unit % 2][:, :]).then_inc(w_hi_ready, 1)

            def g_loads(m, tails, k):
                return m * (G_UNITS // 2) + tails * (WO_UNITS // 2) + k // 2

            def split_g(m, tails, k):
                if not (isinstance(m, int) and m == 0 and k in (0, 1, 4, 5)):
                    if k < 4:
                        act.wait_ge(qk_done, m * QKU + (k - 1))
                    else:
                        act.wait_ge(v_done, m * VU)
                split_hi(g_loads(m, tails, k), k, G_SLOT[k])

            def split_x(b, x):
                if not isinstance(b, int) or b > 0:
                    act.wait_ge(v_done, b * GROUPS * VU)
                act.wait_ge(x_loaded[x % 2], (b * 2 + x // 2 + 1) * 16)
                copy(x_hi[:, 2 * x:2 * x + 2, :], x_raw[x % 2][:, :].rearrange("p (e s) -> p e s", e=2))\
                    .then_inc(x_hi_ready, 1)

            def evacuate_qk(m, u):
                act.wait_ge(qk_done, m * QKU + (u + 1))
                if not (isinstance(m, int) and m == 0):
                    act.wait_ge(qk_ready, m * QKU + (u - QKU + 1))
                copy(qk_raw[u][:, :], u_ps[u % 2][:, :]).then_inc(qk_evacuated, 1)

            def swap_qk(m, u):
                act.wait_ge(qk_evacuated, m * QKU + (u + 1))
                if u >= 2 or not (isinstance(m, int) and m == 0):
                    act.wait_ge(roped, m * QKU + (u - 1))
                for q in range(4):
                    act.dma_start(qk_swap[u % 2][32 * q:32 * q + 32, :],
                                  qk_raw[u][32 * (q ^ 1):32 * (q ^ 1) + 32, :]).then_inc(swapped[u % 2], 16)

            def qk_round(m, u):
                act.wait_ge(roped, m * QKU + (u + 1))
                if not (isinstance(m, int) and m == 0):
                    act.wait_ge(s_done, m * TASKS)
                copy(qk_hi[:, u, :], qk_raw[u][:, :]).then_inc(qk_hi_ready, 1)

            def v_round(m, v):
                act.wait_ge(v_done, m * VU + (v + 1))
                if not (isinstance(m, int) and m == 0):
                    act.wait_ge(pv_done, m * TASKS + ((8 if v == 0 else 16) - TASKS))
                tiles = slice(2, 4) if v == 0 else slice(0, 2)
                copy(v_sb[:, tiles, :, 0:HEAD_DIM],
                     u_ps[v][:, :].rearrange("p (t h d) -> p t h d", t=2, h=GROUP_HEADS)).then_inc(v_hi_ready, 1)

            def exponentiate(n, tau):
                i, j, w = task(tau)
                act.wait_ge(max_done, n * TASKS * 2 + 2 * (tau + 1))
                nc.scalar.activation(prob[tau % 2][:, 0:w], prob[tau % 2][:, 0:w], ACT.Exp,
                                     bias=neg_max[:, tau % 2:tau % 2 + 1], scale=-1.0,
                                     accum_out=row_sum[:, i % 2, j:j + 1]).then_inc(exp_done, 1)

            def pt_round(n, tau):
                w = task(tau)[2]
                act.wait_ge(t_done, n * TASKS + (tau + 1))
                if tau >= 2:
                    act.wait_ge(pv_done, n * TASKS + (tau - 1))
                copy(pt_hi[tau % 2][:, 0:w], t_ps[tau % 2][:, 0:w]).then_inc(pt_hi_ready, 1)

            def o_low(n, c):
                act.wait_ge(pv_done, n * TASKS + GROUP_HEADS * (c + 1))
                copy(o_lo[:, :, :], pv_ps[:, :].rearrange("p (h d) -> p h d", h=GROUP_HEADS)[:, :, HEAD_DIM:])\
                    .then_inc(o_lo_ready, 1)

            def ot_round(b, g, n, c):
                t = TOK_TILES - 1 - c
                act.wait_ge(ott_done, n * TOK_TILES + (c + 1))
                act.wait_ge(consts_ready, 1)
                copy(ot_hi[:, t, bass.ts(g, 2), :],
                     ott_ps[:, 0:2 * P].rearrange("p (e q) -> p e q", e=2)).then_inc(ot_hi_ready, 1)

            def group(n, b, g, m, tails, ahead_m, ahead, new_x):
                for s in range(STEPS + 2):
                    if new_x and s < 2:
                        split_x(b + 1, 2 * s)
                        split_x(b + 1, 2 * s + 1)
                    if m is not None and s % 3 == 0 and 1 <= s // 3 <= QKU:
                        evacuate_qk(m, s // 3 - 1)
                    if n is not None and 1 <= s <= TASKS:
                        pt_round(n, s - 1)
                    if n is not None and s >= 5 and (s - 5) % 4 == 0:
                        o_low(n, (s - 5) // 4)
                    if n is not None and s < TASKS:
                        exponentiate(n, s)
                    if n is not None and s >= 6 and (s - 6) % 4 == 0:
                        ot_round(b, g, n, (s - 6) // 4)
                    if m is not None and s % 3 == 1 and 1 <= s // 3 <= QKU:
                        swap_qk(m, s // 3 - 1)
                    for k, at in SPLIT_STEP.items():
                        if at == s and m is not None:
                            split_g(m, tails, k)
                    for k, at in AHEAD_STEP.items():
                        if at == s and ahead == "group":
                            split_g(ahead_m, tails, k)
                        if at == s and ahead == "wo":
                            act.wait_ge(qk_done, ahead_m * QKU + (k - 1))
                            split_hi(g_loads(ahead_m, tails, k), k, k)
                    if m is not None and s == 15:
                        v_round(m, 0)
                    if m is not None and s in (16, 17):
                        for u in (2 * (s - 16), 2 * (s - 16) + 1):
                            qk_round(m, u)
                    if m is not None and s == 18:
                        v_round(m, 1)

            def prologue():
                split_g(0, 0, 0)
                for x in range(X_UNITS):
                    split_x(0, x)
                split_g(0, 0, 1)
                group(None, 0, 0, 0, 0, 1, "group", False)
                act.wait_ge(tables_loaded, 48)
                copy(scale_sb[:, :], scale_raw[:, :]).then_inc(scale_ready, 1)

            def body(b, g, ahead, fill=True, new_x=False):
                n = b * GROUPS + g
                group(n, b, g, n + 1 if fill else None, b, n + 2, ahead, new_x)

            def tail(b, groups):
                for w in range(2, WO_UNITS):
                    if w < 4:
                        act.wait_ge(v_done, groups * VU)
                    elif w < 7:
                        act.wait_ge(wo_slot_free, b * 6 + (w - 3))
                    else:
                        act.wait_ge(op_done, b * 8 + 4)
                    split_hi(groups * (G_UNITS // 2) + b * (WO_UNITS // 2) + w // 2, w, w % 4)

                def int8_weights(f):
                    if f % 4 < 3:
                        act.wait_ge(wo_slot_free, b * 6 + (f % 4 + 4))
                    else:
                        act.wait_ge(op_done, b * 8 + 8)
                    act.wait_ge(w8_loaded, 16)
                    slot = w_hi[f] if f < 4 else w_lo[f - 4]
                    copy(slot[:, :], w8[:, f, :]).then_inc(w8_ready, 1)

                def x1t_round(t):
                    for k in range(2):
                        act.wait_ge(x1tt_done, b * 8 + (2 * t + k + 1))
                        copy(ot_hi[:, t, 4 * k:4 * k + 4, :], t_ps[k][:, :].rearrange("p (e q) -> p e q", e=4))\
                            .then_inc(x1t_hi_ready, 1)

                for f in range(4):
                    int8_weights(f)
                x1t_round(0)
                for f in range(4, W8_UNITS):
                    int8_weights(f)
                for t in range(1, TOK_TILES):
                    x1t_round(t)
                if groups is not BATCHES * GROUPS:
                    for k in range(2):
                        act.wait_ge(ffn_done, b * 8 + 7)
                        split_hi(groups * (G_UNITS // 2) + (b + 1) * (WO_UNITS // 2) + k // 2, k, k)

            program(body, tail, prologue, act)

        @block.vector
        def _(dve):
            def x_low(b, x):
                dve.wait_ge(x_hi_ready, b * X_UNITS + (x + 1))
                nc.vector.tensor_tensor(x_lo[:, 2 * x:2 * x + 2, :],
                                        x_raw[x % 2][:, :].rearrange("p (e s) -> p e s", e=2),
                                        f32(x_hi[:, 2 * x:2 * x + 2, :]), ALU.subtract).then_inc(x_ready, 1)

            def rotate_cos(m, u):
                dve.wait_ge(swapped[u % 2], (m * 2 + u // 2 + 1) * 64)
                if isinstance(m, int) and m == 0 and u == 0:
                    dve.wait_ge(tables_loaded, 48)
                nc.vector.tensor_tensor(qk_raw[u][:, :], qk_raw[u][:, :], cos_sb[:, :], ALU.mult)\
                    .then_inc(cos_mul, 1)

            def rotate_add(m, u):
                dve.wait_ge(sin_mul, m * QKU + (u + 1))
                dve.wait_ge(cos_mul, m * QKU + (u + 1))
                nc.vector.tensor_tensor(qk_raw[u][:, :], qk_raw[u][:, :], qk_swap[u % 2][:, :], ALU.add)\
                    .then_inc(roped, 1)

            def qk_low(m, u):
                dve.wait_ge(qk_hi_ready, m * QKU + (u + 1))
                nc.vector.tensor_tensor(qk_lo[:, u, :], qk_raw[u][:, :], f32(qk_hi[:, u, :]), ALU.subtract)\
                    .then_inc(qk_ready, 1)

            def v_low(m, v):
                tiles = slice(2, 4) if v == 0 else slice(0, 2)
                dve.wait_ge(v_hi_ready, m * VU + (v + 1))
                nc.vector.tensor_tensor(v_sb[:, tiles, :, HEAD_DIM:],
                                        u_ps[v][:, :].rearrange("p (t h d) -> p t h d", t=2, h=GROUP_HEADS),
                                        f32(v_sb[:, tiles, :, 0:HEAD_DIM]), ALU.subtract).then_inc(v_ready, 1)

            def row_max(n, tau):
                w = task(tau)[2]
                dve.wait_ge(s_done, n * TASKS + (tau + 1))
                nc.vector.memset(turn[:, tau % 2:tau % 2 + 1], 0.0).then_inc(max_done, 1)
                dve.wait_ge(consts_ready, 1)
                nc.vector.tensor_tensor_reduce(out=prob[tau % 2][:, 0:w], in0=s_ps[tau % 2][:, 0:w],
                                               in1=mask[:, SEQ - w:SEQ], scale=-SCALE, scalar=3.0e38,
                                               op0=ALU.add, op1=ALU.min,
                                               accum_out=neg_max[:, tau % 2:tau % 2 + 1]).then_inc(max_done, 1)

            def pt_low(n, tau):
                w = task(tau)[2]
                dve.wait_ge(pt_hi_ready, n * TASKS + (tau + 1))
                nc.vector.tensor_tensor(pt_lo[tau % 2][:, 0:w], t_ps[tau % 2][:, 0:w],
                                        f32(pt_hi[tau % 2][:, 0:w]), ALU.subtract).then_inc(pt_ready, 1)

            def o_normalise(n, c):
                i = TOK_TILES - 1 - c
                o = n * TOK_TILES + (c + 1)
                dve.wait_ge(exp_done, n * TASKS + GROUP_HEADS * (c + 1))
                nc.vector.reciprocal(row_rec[:, :], row_sum[:, i % 2, :]).then_inc(rec_done, 1)
                dve.wait_ge(o_lo_ready, o)
                nc.vector.tensor_tensor(o_sum[:, :, :],
                                        pv_ps[:, :].rearrange("p (h d) -> p h d", h=GROUP_HEADS)[:, :, 0:HEAD_DIM],
                                        o_lo[:, :, :], ALU.add).then_inc(o_sum_done, 1)
                dve.wait_ge(rec_done, o)
                dve.wait_ge(o_sum_done, o)
                nc.vector.tensor_tensor(o_norm[:, :, :], o_sum[:, :, :],
                                        row_rec[:, :].unsqueeze(2).to_broadcast([P, GROUP_HEADS, HEAD_DIM]),
                                        ALU.mult).then_inc(o_ready, 1)

            def ot_low(g, n, c):
                t = TOK_TILES - 1 - c
                dve.wait_ge(ot_hi_ready, n * TOK_TILES + (c + 1))
                nc.vector.tensor_tensor(ot_lo[:, t, bass.ts(g, 2), :],
                                        ott_ps[:, 0:2 * P].rearrange("p (e q) -> p e q", e=2),
                                        f32(ot_hi[:, t, bass.ts(g, 2), :]), ALU.subtract).then_inc(ot_ready, 1)

            def group(n, b, g, m, new_x):
                for s in range(STEPS + 2):
                    if new_x and s < 2:
                        x_low(b + 1, 2 * s)
                        x_low(b + 1, 2 * s + 1)
                    if n is not None and s < TASKS:
                        row_max(n, s)
                    if n is not None and 1 <= s <= TASKS:
                        pt_low(n, s - 1)
                    if n is not None and s >= 5 and (s - 5) % 4 == 0:
                        o_normalise(n, (s - 5) // 4)
                    if n is not None and s >= 6 and (s - 6) % 4 == 0:
                        ot_low(g, n, (s - 6) // 4)
                    if m is not None and s >= 5 and (s - 5) % 3 == 0 and (s - 5) // 3 < QKU:
                        rotate_cos(m, (s - 5) // 3)
                    if m is not None and s >= 6 and (s - 6) % 3 == 0 and (s - 6) // 3 < QKU:
                        rotate_add(m, (s - 6) // 3)
                    if m is not None and s == 15:
                        v_low(m, 0)
                    if m is not None and s in (16, 17):
                        for u in (2 * (s - 16), 2 * (s - 16) + 1):
                            qk_low(m, u)
                    if m is not None and s == 18:
                        v_low(m, 1)

            def prologue():
                for x in range(X_UNITS):
                    x_low(0, x)
                group(None, 0, 0, 0, False)

            def body(b, g, ahead, fill=True, new_x=False):
                n = b * GROUPS + g
                group(n, b, g, n + 1 if fill else None, new_x)

            def tail(b, groups):
                def half_stats(t, h, seen):
                    nc.vector.bn_stats(stats[:, t, 6 * h:6 * h + 6], y[t][:, h * HALF:(h + 1) * HALF])\
                        .then_inc(stats_done, 1)

                def row_stats(which, t, stats_seen):
                    dve.wait_ge(stats_done, b * 16 + stats_seen)
                    nc.vector.memset(turn[:, 2 + t:3 + t], 0.0).then_inc(mv_done, 1)
                    nc.vector.bn_aggr(mean_var[:, t, :], stats[:, t, :]).then_inc(mv_done, 1)
                    dve.wait_ge(mv_done, b * 16 + 2 * (4 * which + t + 1))
                    nc.vector.tensor_scalar(var_eps[:, t:t + 1], mean_var[:, t, 1:2], EPS, None, ALU.add)\
                        .then_inc(ve_done, 1)

                def normalise(which, t, ready):
                    dve.wait_ge(rstd_ready, b * 8 + (4 * which + t + 1))
                    nc.vector.tensor_scalar(y[t][:, :], y[t][:, :], mean_var[:, t, 0:1], rstd[:, t:t + 1],
                                            ALU.subtract, ALU.mult).then_inc(ready, 1)

                for q in range(2 * TOK_TILES):
                    h, t = q // TOK_TILES, q % TOK_TILES
                    if h == 0:
                        dve.wait_ge(y_loaded[t], b * 16 + 16)
                    cols = slice(h * HALF, (h + 1) * HALF)
                    dve.wait_ge(op_done, b * 8 + (q + 1))
                    nc.vector.tensor_tensor(y[t][:, cols], u_ps[q % 2][:, :], y[t][:, cols], ALU.add)\
                        .then_inc(op_added, 1)
                    dve.wait_ge(op_added, b * 8 + (q + 1))
                    half_stats(t, h, None)
                    if h == 1:
                        row_stats(0, t, q + 1)
                        if t >= 1:
                            normalise(0, t - 1, x1_done)
                normalise(0, TOK_TILES - 1, x1_done)

                def x1t_low(t):
                    for k in range(2):
                        dve.wait_ge(x1t_hi_ready, b * 8 + (2 * t + k + 1))
                        nc.vector.tensor_tensor(ot_lo[:, t, 4 * k:4 * k + 4, :],
                                                t_ps[k][:, :].rearrange("p (e q) -> p e q", e=4),
                                                f32(ot_hi[:, t, 4 * k:4 * k + 4, :]), ALU.subtract)\
                            .then_inc(x1t_ready, 1)

                dve.wait_ge(scale_ready, 1)
                x1t_low(0)
                for t in range(TOK_TILES):
                    for h in range(2):
                        q = 2 * t + h + 1
                        cols = slice(h * HALF, (h + 1) * HALF)
                        dve.wait_ge(ffn_done, b * 8 + q)
                        nc.vector.tensor_tensor(z_mul_sb[h][:, :], s_ps[h][:, :], scale_sb[:, cols], ALU.mult)\
                            .then_inc(z_mul, 1)
                        dve.wait_ge(z_mul, b * 8 + q)
                        nc.vector.tensor_tensor(y[t][:, cols], z_mul_sb[h][:, :], y[t][:, cols], ALU.add)\
                            .then_inc(z_added, 1)
                        dve.wait_ge(z_added, b * 8 + q)
                        half_stats(t, h, None)
                        if h == 0 and t + 1 < TOK_TILES:
                            x1t_low(t + 1)
                    row_stats(1, t, 8 + 2 * t + 2)
                    if t >= 1:
                        normalise(1, t - 1, z_done)
                normalise(1, TOK_TILES - 1, z_done)

            program(body, tail, prologue, dve)

        @block.tensor
        def _(pe):
            def three(out_ap, a_hi, a_lo, b_hi, b_lo, first, last):
                nc.tensor.matmul(out_ap, a_hi, b_lo, start=first, stop=False)
                nc.tensor.matmul(out_ap, a_lo, b_hi, start=False, stop=False)
                return nc.tensor.matmul(out_ap, a_hi, b_hi, start=False, stop=last)

            def project_qk(m, tails, u, e, new_x_batch):
                if e == 0:
                    pe.wait_ge(w_ready, g_pos(m, tails) + (u + 1))
                    if u >= 2:
                        pe.wait_ge(qk_evacuated, m * QKU + (u - 1))
                    elif not (isinstance(m, int) and m == 0):
                        pe.wait_ge(v_ready, m * VU + (u - 1))
                if u == 0 and new_x_batch is not None and e % 2 == 0:
                    pe.wait_ge(x_ready, new_x_batch * X_UNITS + (e // 2 + 1))
                slot = G_SLOT[u]
                cols = slice(e * P, (e + 1) * P)
                mm = three(u_ps[u % 2][:, :], w_hi[slot][:, cols], w_lo[slot][:, cols],
                           x_hi[:, e, :], x_lo[:, e, :], e == 0, e == E_TILES - 1)
                if e == E_TILES - 1:
                    mm.then_inc(qk_done, 1)

            def project_v(m, tails, v, half, e):
                t = (2 if v == 0 else 0) + half
                if e == 0 and half == 0:
                    pe.wait_ge(w_ready, g_pos(m, tails) + G_UNITS)
                    pe.wait_ge(qk_evacuated, m * QKU + (3 + v))
                width = GROUP_HEADS * HEAD_DIM
                slot, cols = 2 + e // 4, slice((e % 4) * width, (e % 4 + 1) * width)
                tok = slice(t * P, (t + 1) * P)
                mm = three(u_ps[v][:, half * width:(half + 1) * width], x_hi[:, e, tok], x_lo[:, e, tok],
                           w_hi[slot][:, cols], w_lo[slot][:, cols], e == 0, e == E_TILES - 1)
                if half == 1 and e == E_TILES - 1:
                    mm.then_inc(v_done, 1)

            def fill_pieces(m, tails, new_x_batch):
                pieces = []
                for u in range(QKU):
                    pieces += [(project_qk, (m, tails, u, e, new_x_batch)) for e in range(E_TILES)]
                for v in range(VU):
                    for e2 in range(2 * E_TILES):
                        pieces.append((project_v, (m, tails, v, e2 // E_TILES, e2 % E_TILES)))
                return pieces

            def piece_range(s):
                u, third = s // 3, s % 3
                if u < QKU:
                    cut = [0, 3, 6, 8]
                    return u * 8 + cut[third], u * 8 + cut[third + 1]
                cut = [0, 6, 11, 16]
                return 32 + (u - QKU) * 16 + cut[third], 32 + (u - QKU) * 16 + cut[third + 1]

            def scores(n, b, tau):
                i, j, w = task(tau)
                if tau == 0:
                    pe.wait_ge(qk_ready, n * QKU + 2)
                if tau == 2:
                    pe.wait_ge(qk_ready, n * QKU + 4)
                if tau >= 2:
                    pe.wait_ge(max_done, n * TASKS * 2 + 2 * (tau - 1))
                rows = slice(HEAD_DIM * (j % 2), HEAD_DIM * (j % 2) + HEAD_DIM)
                q, k, tok = 2 * (j // 2), 2 * (j // 2) + 1, slice(i * P, (i + 1) * P)
                three(s_ps[tau % 2][:, 0:w], qk_hi[rows, q, tok], qk_lo[rows, q, tok],
                      qk_hi[rows, k, 0:w], qk_lo[rows, k, 0:w], True, True).then_inc(s_done, 1)

            def transpose_p(n, tau):
                i = task(tau)[0]
                pe.wait_ge(exp_done, n * TASKS + (tau + 1))
                for k in range(i + 1):
                    mm = nc.tensor.transpose(t_ps[tau % 2][:, k * P:(k + 1) * P],
                                             prob[tau % 2][:, k * P:(k + 1) * P], ident[:, :])
                mm.then_inc(t_done, 1)

            def weigh_values(n, tau):
                i, j, _ = task(tau)
                if tau == 0:
                    pe.wait_ge(v_ready, n * VU + VU)
                pe.wait_ge(pt_ready, n * TASKS + (tau + 1))
                o = pv_ps[:, j * P:(j + 1) * P]
                for k in range(i + 1):
                    keys = slice(k * P, (k + 1) * P)
                    nc.tensor.matmul(o, pt_lo[tau % 2][:, keys], v_sb[:, k, j, :], start=k == 0, stop=False)
                    mm = nc.tensor.matmul(o, pt_hi[tau % 2][:, keys], v_sb[:, k, j, :], start=False, stop=k == i)
                mm.then_inc(pv_done, 1)

            def transpose_o(n, c):
                if c >= 1:
                    pe.wait_ge(ot_ready, n * TOK_TILES + c)
                pe.wait_ge(o_ready, n * TOK_TILES + (c + 1))
                flat = o_norm[:, :, :].rearrange("p h d -> p (h d)")
                for k in range(2):
                    mm = nc.tensor.transpose(ott_ps[:, k * P:(k + 1) * P], flat[:, k * P:(k + 1) * P], ident[:, :])
                mm.then_inc(ott_done, 1)

            def group(n, b, m, tails, new_x_batch):
                pieces = fill_pieces(m, tails, new_x_batch) if m is not None else []
                for s in range(STEPS + 1):
                    if n is not None:
                        if s >= 6 and (s - 6) % 4 == 0:
                            transpose_o(n, (s - 6) // 4)
                        if s < TASKS:
                            scores(n, b, s)
                        if 1 <= s <= TASKS:
                            transpose_p(n, s - 1)
                        if 2 <= s <= TASKS + 1:
                            weigh_values(n, s - 2)
                    if m is not None and s < STEPS:
                        first, end = piece_range(s)
                        for work, args in pieces[first:end]:
                            work(*args)

            def prologue():
                pe.wait_ge(consts_ready, 1)
                group(None, 0, 0, 0, 0)

            def body(b, g, ahead, fill=True, new_x=False):
                n = b * GROUPS + g
                group(n, b, n + 1 if fill else None, b, b + 1 if new_x else None)

            def tail(b, groups):
                pe.wait_ge(v_ready, groups * VU)
                pe.wait_ge(ot_ready, b * 16 + 16)
                for q in range(2 * TOK_TILES):
                    h, t = q // TOK_TILES, q % TOK_TILES
                    if q >= 2:
                        pe.wait_ge(op_added, b * 8 + (q - 1))
                    for e in range(E_TILES):
                        w = 4 * h + e // 2
                        if t == 0 and e % 2 == 0:
                            pe.wait_ge(w_ready, wo_pos(groups, b) + (w + 1))
                        cols = slice((e % 2) * HALF, (e % 2 + 1) * HALF)
                        mm = three(u_ps[q % 2][:, :], ot_hi[:, t, e, :], ot_lo[:, t, e, :],
                                   w_hi[w % 4][:, cols], w_lo[w % 4][:, cols], e == 0, e == E_TILES - 1)
                        if t == TOK_TILES - 1 and e in (1, 3, 5):
                            mm.then_inc(wo_slot_free, 1)
                    mm.then_inc(op_done, 1)

                def transpose_x1(t):
                    pe.wait_ge(x1_done, b * TOK_TILES + (t + 1))
                    for e in range(E_TILES):
                        mm = nc.tensor.transpose(t_ps[e // 4][:, (e % 4) * P:(e % 4 + 1) * P],
                                                 y[t][:, e * P:(e + 1) * P], ident[:, :])
                        if e % 4 == 3:
                            mm.then_inc(x1tt_done, 1)

                transpose_x1(0)
                for t in range(TOK_TILES):
                    pe.wait_ge(x1t_ready, b * 8 + (2 * t + 2))
                    for h in range(2):
                        if t >= 1:
                            pe.wait_ge(z_mul, b * 8 + (2 * t + h - 1))
                        for e in range(E_TILES):
                            f = 4 * h + e // 2
                            if t == 0 and e % 2 == 0:
                                pe.wait_ge(w8_ready, b * 8 + (f + 1))
                            slot = w_hi[f] if f < 4 else w_lo[f - 4]
                            cols = slice((e % 2) * HALF, (e % 2 + 1) * HALF)
                            nc.tensor.matmul(s_ps[h][:, :], ot_lo[:, t, e, :], slot[:, cols],
                                             start=e == 0, stop=False)
                            mm = nc.tensor.matmul(s_ps[h][:, :], ot_hi[:, t, e, :], slot[:, cols],
                                                  start=False, stop=e == E_TILES - 1)
                            if t == TOK_TILES - 1 and h == 1 and e in (1, 3, 5):
                                mm.then_inc(w8_free, 1)
                        mm.then_inc(ffn_done, 1)
                        if h == 0 and t + 1 < TOK_TILES:
                            transpose_x1(t + 1)
                pe.wait_ge(z_mul, b * 8 + 8)

            program(body, tail, prologue, pe)


def kernel(**inputs):
    import numpy as np
    import concourse.bacc as bacc
    from concourse.bass_utils import run_bass_kernel_spmd

    x = np.asarray(inputs["L0_attn_hidden_states"])
    wq, wk, wv, wo = (np.asarray(inputs[f"L0_attn_w_{s}"]) for s in ("q", "k", "v", "out"))
    w8 = np.asarray(inputs["L0_ffn_weight"])
    scales = np.asarray(inputs["L0_ffn_scales"])

    x_units = x.transpose(0, 2, 1).reshape(BATCHES, X_UNITS, 2, P, SEQ).transpose(0, 1, 3, 2, 4)
    x_units = x_units.reshape(BATCHES * X_UNITS, P, UNIT)

    def qk_unit(w, g, pair):
        rows = w[(GROUP_HEADS * g + 2 * pair) * HEAD_DIM:][:2 * HEAD_DIM]
        rows = rows.reshape(2, HEAD_DIM // 2, 2, EMBED).transpose(0, 2, 1, 3).reshape(P, E_TILES, P)
        return rows.transpose(2, 1, 0).reshape(P, UNIT)

    def v_unit(g, half):
        width = GROUP_HEADS * HEAD_DIM
        rows = wv[g * width:(g + 1) * width].reshape(width, E_TILES, P)[:, 4 * half:4 * half + 4]
        return rows.transpose(2, 1, 0).reshape(P, UNIT)

    def out_unit(w, u):
        h, e = u // 4, 2 * (u % 4)
        rows = w[h * HALF:(h + 1) * HALF].reshape(HALF, E_TILES, P)[:, e:e + 2]
        return rows.transpose(2, 1, 0).reshape(P, UNIT)

    units = []
    for g in [1, 2, 3, 0]:
        units += [qk_unit(wq, g, 0), qk_unit(wk, g, 0), qk_unit(wq, g, 1), qk_unit(wk, g, 1)]
        units += [v_unit(g, 0), v_unit(g, 1)]
    units += [out_unit(wo, u) for u in range(WO_UNITS)]
    w_units = np.stack(units)
    w8_units = np.stack([out_unit(w8, u) for u in range(W8_UNITS)], axis=1).reshape(P, W8_UNITS * UNIT)
    w8_units = np.ascontiguousarray(w8_units).view(np.int32)

    freq = (np.float32(1.0) / np.float32(10000.0) ** (np.arange(0, HEAD_DIM, 2, dtype=np.float32)
                                                       / np.float32(HEAD_DIM))).astype(np.float32)
    angle = (np.arange(SEQ, dtype=np.float32)[None, :] * freq[:, None]).astype(np.float32)
    cos32, sin32 = np.cos(angle), np.sin(angle)
    cos_table = np.concatenate([cos32, cos32, cos32, cos32])
    sin_table = np.concatenate([-sin32, sin32, -sin32, sin32])

    arrays = {
        "x_units": x_units, "x_rows": x.reshape(BATCHES * TOK_TILES, P, EMBED), "w_units": w_units,
        "w8_units": w8_units, "scales": scales.reshape(EMBED), "cos_table": cos_table, "sin_table": sin_table,
    }
    arrays = {k: np.ascontiguousarray(v) for k, v in arrays.items()}
    nc = bacc.Bacc("TRN2", target_bir_lowering=False, num_devices=1)
    args = [nc.dram_tensor(k, v.shape, mybir.dt.from_np(v.dtype), kind="ExternalInput").ap()
            for k, v in arrays.items()]
    out = nc.dram_tensor("out", (BATCHES * TOK_TILES, P, EMBED), F32, kind="ExternalOutput").ap()
    layer_program(nc, *args, out)
    result = run_bass_kernel_spmd(nc, [arrays], core_ids=[0])
    return result.results[0]["out"].reshape(BATCHES, SEQ, EMBED)
```

```python
from contextlib import ExitStack

import concourse.bass as bass
from concourse import mybir

F32 = mybir.dt.float32
F32R = mybir.dt.float32r
F16 = mybir.dt.float16
I8 = mybir.dt.int8
I32 = mybir.dt.int32
ACT = mybir.ActivationFunctionType
ALU = mybir.AluOpType

P = 128
BATCHES, SEQ, EMBED = 4, 512, 1024
HEADS, HEAD_DIM = 16, 64
GROUPS = 4
GROUP_HEADS = HEADS // GROUPS
TOK_TILES = SEQ // P
E_TILES = EMBED // P
TASKS = TOK_TILES * GROUP_HEADS
UNIT = 1024
G_UNITS, WO_UNITS, W8_UNITS, X_UNITS = 6, 8, 8, 4
HALF = EMBED // 2
SCALE = float(HEAD_DIM) ** -0.5
MASKED = -1.0e30
EPS = 1e-05
QKU, VU = 4, 2
ROUNDS = 2 * (2 + 4)
PAIRS = TASKS // 2
UNITS = TASKS // 4
STEPS = TASKS + 4


def layer_program(nc, x_units, x_rows, w_units, w8_units, scales, cos_table, sin_table, out):
    ctx = ExitStack()
    with ctx:
        def sb(name, shape, dt=F32):
            return ctx.enter_context(nc.sbuf_tensor(name, shape, dt))

        def pb(name):
            return ctx.enter_context(nc.psum_tensor(name, [P, 512], F32))

        def sem(name):
            return ctx.enter_context(nc.semaphore(name))

        w_raw = [sb(f"w_raw{i}", [P, UNIT]) for i in range(2)]
        w_hi = [sb(f"w_hi{i}", [P, UNIT], F32R) for i in range(4)]
        w_lo = [sb(f"w_lo{i}", [P, UNIT], F32R) for i in range(4)]
        x_hi = sb("x_hi", [P, E_TILES, SEQ], F32R)
        x_lo = sb("x_lo", [P, E_TILES, SEQ], F32R)
        ot_hi = sb("ot_hi", [P, TOK_TILES, E_TILES, P], F32R)
        ot_lo = sb("ot_lo", [P, TOK_TILES, E_TILES, P], F32R)
        y = [sb(f"y{t}", [P, EMBED]) for t in range(TOK_TILES)]
        q_st = sb("q_st", [P, GROUP_HEADS, SEQ], F32R)
        k_st = sb("k_st", [P, GROUP_HEADS, SEQ], F32R)
        k_lo = sb("k_lo", [P, GROUP_HEADS // 2, SEQ], F32R)
        qk_raw = [sb(f"qk_raw{u}", [P, SEQ]) for u in range(QKU)]
        w8_words = [raw[:, :].bitcast(I32) for raw in qk_raw]
        w8 = [words.bitcast(I8).rearrange("p (u c) -> p u c", u=2) for words in w8_words]
        qk_swap = [sb(f"qk_swap{i}", [P, SEQ]) for i in range(2)]
        cos_sb = sb("cos_sb", [P, SEQ])
        sin_sb = sb("sin_sb", [P, SEQ])
        v_sb = sb("v_sb", [P, TOK_TILES, GROUP_HEADS, 2 * HEAD_DIM], F32R)
        prob = [sb(f"prob{i}", [P, SEQ]) for i in range(3)]
        pt_hi = [sb(f"pt_hi{i}", [P, TOK_TILES, 2 * P], F32R) for i in range(2)]
        pt_lo = [sb(f"pt_lo{i}", [P, TOK_TILES, 2 * P], F32R) for i in range(2)]
        o_part = sb("o_part", [P, 2 * P])
        o_sum = sb("o_sum", [P, 2 * P])
        mask = sb("mask", [P, SEQ])
        ident = sb("ident", [P, P])
        scale_sb = sb("scale_sb", [P, EMBED])
        scale_raw = prob[2][:, :].bitcast(F16)
        z_mul_sb = prob[0:2]
        neg_max = sb("neg_max", [P, 2])
        row_sum = sb("row_sum", [P, 2])
        row_rec = sb("row_rec", [P, 2])
        stats = sb("stats", [P, TOK_TILES, 12])
        mean_var = sb("mean_var", [P, TOK_TILES, 2])
        var_eps = sb("var_eps", [P, TOK_TILES])
        rstd = sb("rstd", [P, TOK_TILES])
        minus_half = sb("minus_half", [P, 1])
        turn = sb("turn", [P, 2 + TOK_TILES])

        u_ps = [pb("u_ps0"), pb("u_ps1")]
        s_ps = [pb("s_ps0"), pb("s_ps1")]
        t_ps = [pb("t_ps0"), pb("t_ps1")]
        o_ps = [pb("o_ps0"), pb("o_ps1")]
        op_ps = [s_ps + u_ps, t_ps + o_ps]

        w_loaded = [sem(f"w_loaded{i}") for i in range(2)]
        x_loaded = [sem(f"x_loaded{x}") for x in range(X_UNITS)]
        y_loaded = [sem(f"y_loaded{t}") for t in range(TOK_TILES)]
        stored = [sem(f"stored{t}") for t in range(TOK_TILES)]
        swapped = [sem(f"swapped{i}") for i in range(2)]
        tables_loaded = sem("tables_loaded")
        w8_loaded = sem("w8_loaded")
        consts_ready = sem("consts_ready")
        consts_step = sem("consts_step")
        scale_ready = sem("scale_ready")
        w_hi_ready, w_ready = sem("w_hi_ready"), sem("w_ready")
        x_used = sem("x_used")
        x_hi_ready = [sem(f"x_hi_ready{x}") for x in range(X_UNITS)]
        x_ready = [sem(f"x_ready{x}") for x in range(X_UNITS)]
        qk_done, v_done = sem("qk_done"), sem("v_done")
        qk_evacuated = sem("qk_evacuated")
        sin_mul, cos_mul, roped = sem("sin_mul"), sem("cos_mul"), sem("roped")
        qk_hi_ready, q_ready, k_ready = sem("qk_hi_ready"), sem("q_ready"), sem("k_ready")
        v_hi_ready, v_ready = sem("v_hi_ready"), sem("v_ready")
        s_done, max_done, exp_done = sem("s_done"), sem("max_done"), sem("exp_done")
        t_done, pt_hi_ready, pt_ready = sem("t_done"), sem("pt_hi_ready"), sem("pt_ready")
        rec_done, norm_done = sem("rec_done"), sem("norm_done")
        pv_done, o_part_ready, o_sum_done = sem("pv_done"), sem("o_part_ready"), sem("o_sum_done")
        ot_hi_ready, ot_ready = sem("ot_hi_ready"), sem("ot_ready")
        wo_slot_free, op_done, op_added = sem("wo_slot_free"), sem("op_done"), sem("op_added")
        stats_done, mv_done, ve_done = sem("stats_done"), sem("mv_done"), sem("ve_done")
        rstd_ready, x1_done = sem("rstd_ready"), sem("x1_done")
        x1tt_done, x1t_hi_ready, x1t_ready = sem("x1tt_done"), sem("x1t_hi_ready"), sem("x1t_ready")
        w8_ready, w8_free, ffn_done = sem("w8_ready"), sem("w8_free"), sem("ffn_done")
        z_mul, z_added, z_done = sem("z_mul"), sem("z_added"), sem("z_done")

        block = ctx.enter_context(nc.Block())

        def f32(ap):
            return ap.bitcast(F32)

        def task(tau):
            i = TOK_TILES - 1 - 2 * (tau // PAIRS) - tau % 2
            return i, tau // 2 % GROUP_HEADS, P * (i + 1)

        def unit_tiles(w):
            return slice(2, 4) if w < UNITS // 2 else slice(0, 2)

        def v_parts(tiles, part):
            blocks = v_sb[:, tiles, :, :].rearrange("p t (a j) (c d) -> p (t a) (j c) d", j=2, c=2)
            return blocks[:, :, 0:4:3, :] if part == "hi" else blocks[:, :, 1:3, :]

        def head_rows(j):
            return slice(j * HEAD_DIM, (j + 1) * HEAD_DIM), slice(j * 2 * P, (j + 1) * 2 * P)

        def g_pos(m, tails):
            return m * G_UNITS + tails * WO_UNITS

        def wo_pos(groups, b):
            return groups * G_UNITS + b * WO_UNITS

        G_SLOT = [0, 1, 0, 1, 2, 3]
        SPLIT_STEP = {2: 4, 3: 7, 4: 8, 5: 11}
        AHEAD_STEP = {0: 13, 1: 16}

        ROUND_STEP = {12: [(0, 0)], 13: [(0, 1)], 14: [(1, 0)], 15: [(1, 1)],
                      17: [(2, 0), (2, 1)], 18: [(3, 0), (3, 1)]}
        EARLY_OUT = [(u, t) for t in (2, 3) for u in range(2)]
        EARLY_STEP = [0, 0, 1, 1, 9, 10, 11, 12]
        DVE_SPLIT = (3, 5)
        W8_ORDER = [0, 4, 1, 5, 2, 3, 6, 7]

        def program(body, tail, prologue, eng):
            prologue()
            with eng.Fori(0, BATCHES - 1) as b:
                with eng.Fori(0, GROUPS - 2) as g:
                    body(b, g, ahead="group")
                body(b, GROUPS - 2, ahead="group", last_x=True)
                body(b, GROUPS - 1, ahead="wo", new_x=True)
                tail(b, b * GROUPS + (GROUPS + 1))
            last = BATCHES - 1
            with eng.Fori(0, GROUPS - 2) as g:
                body(last, g, ahead="group")
            body(last, GROUPS - 2, ahead="wo")
            body(last, GROUPS - 1, ahead=None, fill=False)
            tail(last, BATCHES * GROUPS)

        @block.sync
        def _(sp):
            def load_w(row, pos, unit):
                i = unit % 2
                sp.wait_ge(w_ready, pos - 1)
                sp.wait_ge(consts_ready, 1)
                sp.dma_start(w_raw[i][:, :], w_units[row, :, :]).then_inc(w_loaded[i], 16)

            def load_x(b, x):
                sp.dma_start(y[x][:, :], x_units[b * X_UNITS + x, :, :]).then_inc(x_loaded[x], 16)

            def swap_qk(m, u):
                sp.wait_ge(qk_evacuated, m * QKU + (u + 1))
                for q in range(4):
                    sp.dma_start(qk_swap[u % 2][32 * q:32 * q + 32, :],
                                  qk_raw[u][32 * (q ^ 1):32 * (q ^ 1) + 32, :]).then_inc(swapped[u % 2], 16)

            def loads(g, m, tails, ahead):
                def unit(k):
                    load_w(g * G_UNITS + k, g_pos(m, tails) + k, k)

                def unit_ahead(k):
                    if ahead:
                        row = {"wo": GROUPS, "first": 0}.get(ahead, g + 1) * G_UNITS
                        load_w(row + k, g_pos(m + 1, tails) + k, k)

                unit(2)
                unit(3)
                swap_qk(m, 0)
                unit(4)
                swap_qk(m, 1)
                unit(5)
                swap_qk(m, 2)
                unit_ahead(0)
                unit_ahead(1)
                swap_qk(m, 3)

            def load_rows(b, t):
                sp.dma_start(y[t][:, :], x_rows[b * TOK_TILES + t, :, :]).then_inc(y_loaded[t], 16)

            def prologue():
                g0 = (GROUPS - 1) * G_UNITS
                sp.dma_start(w_raw[0][:, :], w_units[g0, :, :]).then_inc(w_loaded[0], 16)
                for x in range(3):
                    load_x(0, x)
                sp.dma_start(w_raw[1][:, :], w_units[g0 + 1, :, :]).then_inc(w_loaded[1], 16)
                load_x(0, 3)
                sp.dma_start(cos_sb[:, :], cos_table).then_inc(tables_loaded, 16)
                sp.dma_start(sin_sb[:, :], sin_table).then_inc(tables_loaded, 16)
                sp.dma_start(scale_raw, scales.partition_broadcast(P)).then_inc(tables_loaded, 16)
                loads(GROUPS - 1, 0, 0, "first")
                for x in range(X_UNITS):
                    sp.wait_ge(x_ready[x], 1)

            def body(b, g, ahead, fill=True, new_x=False, last_x=False):
                n = b * GROUPS + g
                m, tails = n + 1, b
                if last_x:
                    for x in range(X_UNITS):
                        load_x(b + 1, x)
                if fill:
                    loads(g, m, tails, ahead)
                if ahead == "wo":
                    for t in range(TOK_TILES):
                        load_rows(b, t)

            def tail(b, groups):
                for w in range(2, WO_UNITS):
                    if w == 4:
                        sp.wait_ge(q_ready, groups * GROUP_HEADS)
                        sp.wait_ge(consts_ready, 1)
                        sp.wait_ge(k_ready, groups * GROUP_HEADS)
                        sp.wait_ge(consts_ready, 1)
                        for i in range(QKU):
                            sp.dma_start(w8_words[i], w8_units[i, :, :]).then_inc(w8_loaded, 16)
                    load_w(GROUPS * G_UNITS + w, wo_pos(groups, b) + w, w)
                if groups is not BATCHES * GROUPS:
                    for k in range(2):
                        load_w(k, wo_pos(groups, b) + WO_UNITS + k, k)
                for t in range(TOK_TILES):
                    sp.wait_ge(z_done, b * TOK_TILES + (t + 1))
                    sp.wait_ge(consts_ready, 1)
                    sp.dma_start(out[b * TOK_TILES + t, :, :], y[t][:, :]).then_inc(stored[t], 16)

            program(body, tail, prologue, sp)
            for t in range(TOK_TILES):
                sp.wait_ge(stored[t], BATCHES * 16)

        @block.gpsimd
        def _(pool):
            def split_lo(pos, unit, slot):
                pool.wait_ge(w_hi_ready, pos + 1)
                if isinstance(pos, int) and pos in (4, 6):
                    pool.wait_ge(w_ready, pos)
                nc.gpsimd.tensor_tensor(w_lo[slot][:, :], w_raw[unit % 2][:, :], f32(w_hi[slot][:, :]),
                                        ALU.subtract).then_inc(w_ready, 1)

            def rotate(m, u):
                pool.wait_ge(swapped[u % 2], (m * 2 + u // 2 + 1) * 64)
                if isinstance(m, int) and m == 0 and u == 0:
                    pool.wait_ge(tables_loaded, 48)
                nc.gpsimd.tensor_tensor(qk_swap[u % 2][:, :], qk_swap[u % 2][:, :], sin_sb[:, :],
                                        ALU.mult).then_inc(sin_mul, 1)
                nc.gpsimd.tensor_tensor(qk_raw[u][:, :], qk_raw[u][:, :], cos_sb[:, :], ALU.mult)\
                    .then_inc(cos_mul, 1)
                pool.wait_ge(sin_mul, m * QKU + (u + 1))
                pool.wait_ge(cos_mul, m * QKU + (u + 1))
                nc.gpsimd.tensor_tensor(qk_raw[u][:, :], qk_raw[u][:, :], qk_swap[u % 2][:, :], ALU.add)\
                    .then_inc(roped, 1)

            def x_low(b, x):
                pool.wait_ge(x_hi_ready[x], b + 1)
                nc.gpsimd.tensor_tensor(x_lo[:, 2 * x:2 * x + 2, :],
                                        y[x][:, :].rearrange("p (e s) -> p e s", e=2),
                                        f32(x_hi[:, 2 * x:2 * x + 2, :]), ALU.subtract).then_inc(x_ready[x], 1)

            def group(b, m, tails, ahead_m, ahead, last_x):
                for s in range(STEPS + 2):
                    for k, at in SPLIT_STEP.items():
                        if at == s and m is not None and not (isinstance(m, int) and m == 0 and k in DVE_SPLIT):
                            split_lo(g_pos(m, tails) + k, k, G_SLOT[k])
                    for k, at in AHEAD_STEP.items():
                        if at == s and ahead:
                            split_lo(g_pos(ahead_m, tails) + k, k, k)
                    if s >= 6 and s % 3 == 0 and (s - 6) // 3 < QKU and m is not None:
                        rotate(m, (s - 6) // 3)
                    if last_x and s in (19, 21):
                        x_low(b + 1, s - 18)

            def prologue():
                nc.gpsimd.memset(mask[:, :], 0.0).then_inc(consts_step, 1)
                nc.gpsimd.memset(ident[:, :], 0.0).then_inc(consts_step, 1)
                nc.gpsimd.memset(minus_half[:, :], -0.5).then_inc(consts_step, 1)
                pool.wait_ge(consts_step, 3)
                nc.gpsimd.affine_select(out=mask[:, SEQ - P:SEQ], in_=mask[:, SEQ - P:SEQ],
                                        compare_op=ALU.is_ge, fill=MASKED, base=0, pattern=[[-1, P]],
                                        channel_multiplier=1).then_inc(consts_step, 1)
                nc.gpsimd.affine_select(out=ident[:, :], in_=ident[:, :], compare_op=ALU.not_equal, fill=1.0,
                                        base=0, pattern=[[-1, P]], channel_multiplier=1).then_inc(consts_step, 1)
                pool.wait_ge(consts_step, 5)
                nc.gpsimd.memset(turn[:, :], 0.0).then_inc(consts_ready, 1)
                for k in range(2):
                    split_lo(k, k, k)
                group(0, 0, 0, 1, "group", False)

            def body(b, g, ahead, fill=True, new_x=False, last_x=False):
                n = b * GROUPS + g
                group(b, n + 1 if fill else None, b, n + 2, ahead, last_x)

            def tail(b, groups):
                for w in range(2, WO_UNITS):
                    split_lo(wo_pos(groups, b) + w, w, w % 4)

                def rsqrt(which, t):
                    pool.wait_ge(ve_done, b * 8 + (4 * which + t + 1))
                    nc.gpsimd.tensor_tensor(rstd[:, t:t + 1], var_eps[:, t:t + 1], minus_half[:, :],
                                            ALU.pow).then_inc(rstd_ready, 1)
                for t in range(TOK_TILES):
                    rsqrt(0, t)
                for t in range(TOK_TILES - 1):
                    rsqrt(1, t)
                if groups is not BATCHES * GROUPS:
                    for k in range(2):
                        pool.wait_ge(w8_free, b * 3 + (k + 1))
                        split_lo(wo_pos(groups, b) + WO_UNITS + k, k, k)
                rsqrt(1, TOK_TILES - 1)
                if groups is not BATCHES * GROUPS:
                    for t in range(TOK_TILES):
                        pool.wait_ge(stored[t], b * 16 + 16)

            program(body, tail, prologue, pool)

        @block.scalar
        def _(act):
            def copy(dst, src):
                return nc.scalar.activation(dst, src, ACT.Copy)

            def split_hi(loads, unit, slot):
                act.wait_ge(w_loaded[unit % 2], (loads + 1) * 16)
                copy(w_hi[slot][:, :], w_raw[unit % 2][:, :]).then_inc(w_hi_ready, 1)

            def g_loads(m, tails, k):
                return m * (G_UNITS // 2) + tails * (WO_UNITS // 2) + k // 2

            def split_g(m, tails, k):
                if not (isinstance(m, int) and m == 0 and k in (0, 1, 4, 5)):
                    if k < 4:
                        act.wait_ge(qk_done, m * QKU + (k - 1))
                    else:
                        act.wait_ge(v_done, m * VU)
                split_hi(g_loads(m, tails, k), k, G_SLOT[k])

            def split_x(b, x):
                if not isinstance(b, int) or b > 0:
                    if x < X_UNITS - 1:
                        act.wait_ge(x_used, (b * GROUPS - 1) * 3 + (x + 1))
                    else:
                        act.wait_ge(v_done, b * GROUPS * VU)
                act.wait_ge(x_loaded[x], b * 16 + 16)
                copy(x_hi[:, 2 * x:2 * x + 2, :], y[x][:, :].rearrange("p (e s) -> p e s", e=2))\
                    .then_inc(x_hi_ready[x], 1)

            def evacuate_qk(m, u):
                act.wait_ge(qk_done, m * QKU + (u + 1))
                if u >= 2:
                    act.wait_ge(roped, m * QKU + (u - 1))
                elif not (isinstance(m, int) and m == 0):
                    act.wait_ge(q_ready, m * GROUP_HEADS)
                    act.wait_ge(k_ready, m * GROUP_HEADS)
                copy(qk_raw[u][:, :], u_ps[u % 2][:, :]).then_inc(qk_evacuated, 1)

            def qk_round(m, u, j):
                act.wait_ge(roped, m * QKU + (u + 1))
                if not (isinstance(m, int) and m == 0):
                    act.wait_ge(s_done, m * TASKS - (4 if u < 2 else 0))
                rows, other, head = head_rows(j)[0], head_rows(1 - j)[0], u // 2 * 2 + j
                for to in ([rows] if u % 2 == 0 else [rows, other]):
                    place = (q_st if u % 2 == 0 else k_st)[to, head, :]
                    copy(place, qk_raw[u][rows, :]).then_inc(qk_hi_ready, 1)

            def v_round(m, v):
                act.wait_ge(v_done, m * VU + (v + 1))
                if not (isinstance(m, int) and m == 0):
                    act.wait_ge(pv_done, m * PAIRS + ((4 if v == 0 else 8) - PAIRS))
                tiles = slice(2, 4) if v == 0 else slice(0, 2)
                copy(v_parts(tiles, "hi"), u_ps[v][:, :].rearrange("p (a j d) -> p a j d", j=2, d=HEAD_DIM))\
                    .then_inc(v_hi_ready, 1)

            def exponentiate(n, tau):
                w = task(tau)[2]
                act.wait_ge(max_done, n * TASKS * 2 + 2 * (tau + 1))
                nc.scalar.activation(prob[tau % 3][:, 0:w], prob[tau % 3][:, 0:w], ACT.Exp,
                                     bias=neg_max[:, tau % 2:tau % 2 + 1], scale=-1.0,
                                     accum_out=row_sum[:, tau % 2:tau % 2 + 1]).then_inc(exp_done, 1)

            def pt_round(n, tau):
                i, p = task(tau)[0], tau // 2
                act.wait_ge(t_done, n * TASKS + (tau + 1))
                if p >= 2 and tau % 2 == 0:
                    act.wait_ge(pv_done, n * PAIRS + (p - 1))
                copy(pt_hi[p % 2][:, 0:i + 1, i % 2 * P:i % 2 * P + P],
                     t_ps[tau % 2][:, 0:(i + 1) * P].rearrange("p (k q) -> p k q", q=P)).then_inc(pt_hi_ready, 1)

            def o_move(n, w):
                act.wait_ge(pv_done, n * PAIRS + (2 * w + 2))
                for j in range(2):
                    rows, cols = head_rows(j)
                    copy(o_part[rows, :], o_ps[w % 2][head_rows(1 - j)[0], cols]).then_inc(o_part_ready, 1)

            def ot_round(g, n, w):
                act.wait_ge(o_sum_done, n * UNITS * 2 + (2 * w + 2))
                act.wait_ge(consts_ready, 1)
                copy(ot_hi[:, unit_tiles(w), bass.ds(g * 2 + w % 2, 1), :].rearrange("p t e q -> p t (e q)"),
                     o_sum[:, :].rearrange("p (t q) -> p t q", q=P)).then_inc(ot_hi_ready, 1)

            def group(n, b, g, m, tails, ahead_m, ahead, last_x):
                for s in range(STEPS + 2):
                    if m is not None and s % 3 == 0 and 1 <= s // 3 <= QKU:
                        evacuate_qk(m, s // 3 - 1)
                    if n is not None and 2 <= s < TASKS + 2:
                        pt_round(n, s - 2)
                    if n is not None and s < TASKS:
                        exponentiate(n, s)
                    if n is not None and s >= 8 and s % 4 == 0:
                        o_move(n, (s - 8) // 4)
                    if n is not None and s >= 9 and s % 4 == 1:
                        ot_round(g, n, (s - 9) // 4)
                    for k, at in SPLIT_STEP.items():
                        if at == s and m is not None:
                            split_g(m, tails, k)
                    for k, at in AHEAD_STEP.items():
                        if at == s and ahead == "group":
                            split_g(ahead_m, tails, k)
                        if at == s and ahead == "wo":
                            act.wait_ge(qk_done, ahead_m * QKU + (k - 1))
                            split_hi(g_loads(ahead_m, tails, k), k, k)
                    if last_x and s in (18, 20):
                        split_x(b + 1, s - 17)
                    if m is not None and s == 17:
                        v_round(m, 0)
                    if m is not None:
                        for u, j in ROUND_STEP.get(s, []):
                            qk_round(m, u, j)
                    if m is not None and s == STEPS:
                        v_round(m, 1)

            def prologue():
                split_g(0, 0, 0)
                split_x(0, 1)
                split_g(0, 0, 1)
                split_x(0, 3)
                group(None, 0, 0, 0, 0, 1, "group", False)
                act.wait_ge(tables_loaded, 48)
                copy(scale_sb[:, :], scale_raw).then_inc(scale_ready, 1)

            def body(b, g, ahead, fill=True, new_x=False, last_x=False):
                n = b * GROUPS + g
                group(n, b, g, n + 1 if fill else None, b, n + 2, ahead, last_x)

            def tail(b, groups):
                for w in range(2, WO_UNITS):
                    if w < 4:
                        act.wait_ge(v_done, groups * VU)
                    elif w < 7:
                        act.wait_ge(wo_slot_free, b * 5 + (w - 3))
                    else:
                        act.wait_ge(op_done, b * 8 + 4)
                    split_hi(groups * (G_UNITS // 2) + b * (WO_UNITS // 2) + w // 2, w, w % 4)

                def int8_weights(f):
                    if f % 4 < 2:
                        act.wait_ge(wo_slot_free, b * 5 + (f % 4 + 4))
                    else:
                        act.wait_ge(op_done, b * 8 + 8)
                    act.wait_ge(w8_loaded, b * 64 + 64)
                    slot = w_hi[f] if f < 4 else w_lo[f - 4]
                    copy(slot[:, :], w8[f // 2][:, f % 2, :]).then_inc(w8_ready, 1)

                def x1t_round(t):
                    for k in range(2):
                        act.wait_ge(x1tt_done, b * 8 + (2 * t + k + 1))
                        copy(ot_hi[:, t, 4 * k:4 * k + 4, :], u_ps[k][:, :].rearrange("p (e q) -> p e q", e=4))\
                            .then_inc(x1t_hi_ready, 1)

                for f in W8_ORDER[:4]:
                    int8_weights(f)
                x1t_round(0)
                for f in W8_ORDER[4:]:
                    int8_weights(f)
                for t in range(1, TOK_TILES):
                    x1t_round(t)
                if groups is not BATCHES * GROUPS:
                    for k in range(2):
                        act.wait_ge(ffn_done, b * 8 + 7)
                        split_hi(groups * (G_UNITS // 2) + (b + 1) * (WO_UNITS // 2) + k // 2, k, k)

            program(body, tail, prologue, act)

        @block.vector
        def _(dve):
            def x_round(b, x):
                if not isinstance(b, int) or b > 0:
                    if x < X_UNITS - 1:
                        dve.wait_ge(x_used, (b * GROUPS - 1) * 3 + (x + 1))
                    else:
                        dve.wait_ge(v_done, b * GROUPS * VU)
                dve.wait_ge(x_loaded[x], b * 16 + 16)
                nc.vector.tensor_copy(x_hi[:, 2 * x:2 * x + 2, :], y[x][:, :].rearrange("p (e s) -> p e s", e=2))\
                    .then_inc(x_hi_ready[x], 1)

            def x_low(b, x):
                dve.wait_ge(x_hi_ready[x], b + 1)
                nc.vector.tensor_tensor(x_lo[:, 2 * x:2 * x + 2, :],
                                        y[x][:, :].rearrange("p (e s) -> p e s", e=2),
                                        f32(x_hi[:, 2 * x:2 * x + 2, :]), ALU.subtract).then_inc(x_ready[x], 1)

            def first_split_lo(k):
                dve.wait_ge(w_hi_ready, k + 1)
                dve.wait_ge(w_ready, k)
                nc.vector.tensor_tensor(w_lo[G_SLOT[k]][:, :], w_raw[k % 2][:, :], f32(w_hi[G_SLOT[k]][:, :]),
                                        ALU.subtract).then_inc(w_ready, 1)

            def qk_low(m, u, j):
                rows, other, head = head_rows(j)[0], head_rows(1 - j)[0], u // 2 * 2 + j
                if u % 2 == 0:
                    hi, lo, seen, ready = q_st[rows, head, :], q_st[other, head, :], j + 1, q_ready
                else:
                    hi, lo, seen, ready = k_st[rows, head, :], k_lo[rows, u // 2, :], 2 + 2 * j + 2, k_ready
                dve.wait_ge(qk_hi_ready, m * ROUNDS + (ROUNDS // 2 * (u // 2) + seen))
                nc.vector.tensor_tensor(lo, qk_raw[u][rows, :], f32(hi), ALU.subtract).then_inc(ready, 1)

            def v_low(m, v):
                tiles = slice(2, 4) if v == 0 else slice(0, 2)
                dve.wait_ge(v_hi_ready, m * VU + (v + 1))
                nc.vector.tensor_tensor(v_parts(tiles, "lo"),
                                        u_ps[v][:, :].rearrange("p (a j d) -> p a j d", j=2, d=HEAD_DIM),
                                        f32(v_parts(tiles, "hi")), ALU.subtract).then_inc(v_ready, 1)

            def row_max(n, tau):
                w = task(tau)[2]
                dve.wait_ge(s_done, n * TASKS + (tau + 1))
                nc.vector.memset(turn[:, tau % 2:tau % 2 + 1], 0.0).then_inc(max_done, 1)
                dve.wait_ge(consts_ready, 1)
                nc.vector.tensor_tensor_reduce(out=prob[tau % 3][:, 0:w], in0=s_ps[tau % 2][:, 0:w],
                                               in1=mask[:, SEQ - w:SEQ], scale=-SCALE, scalar=3.0e38,
                                               op0=ALU.add, op1=ALU.min,
                                               accum_out=neg_max[:, tau % 2:tau % 2 + 1]).then_inc(max_done, 1)

            def normalise_p(n, tau):
                dve.wait_ge(exp_done, n * TASKS + (tau + 1))
                w, col = task(tau)[2], slice(tau % 2, tau % 2 + 1)
                nc.vector.reciprocal(row_rec[:, col], row_sum[:, col]).then_inc(rec_done, 1)
                dve.wait_ge(rec_done, n * TASKS + (tau + 1))
                nc.vector.tensor_scalar(prob[tau % 3][:, 0:w], prob[tau % 3][:, 0:w], row_rec[:, col], None,
                                        ALU.mult).then_inc(norm_done, 1)

            def pt_low(n, tau):
                i, p = task(tau)[0], tau // 2
                block = (slice(None), slice(0, i + 1), slice(i % 2 * P, i % 2 * P + P))
                dve.wait_ge(pt_hi_ready, n * TASKS + (tau + 1))
                nc.vector.tensor_tensor(pt_lo[p % 2][block],
                                        t_ps[tau % 2][:, 0:(i + 1) * P].rearrange("p (k q) -> p k q", q=P),
                                        f32(pt_hi[p % 2][block]), ALU.subtract).then_inc(pt_ready, 1)

            def o_add(n, w):
                if w >= 1:
                    dve.wait_ge(ot_ready, n * UNITS + w)
                dve.wait_ge(o_part_ready, n * UNITS * 2 + (2 * w + 2))
                for j in range(2):
                    rows, cols = head_rows(j)
                    nc.vector.tensor_tensor(o_sum[rows, :], o_ps[w % 2][rows, cols], o_part[rows, :], ALU.add)\
                        .then_inc(o_sum_done, 1)

            def ot_low(g, n, w):
                block = (slice(None), unit_tiles(w), bass.ds(g * 2 + w % 2, 1), slice(None))
                dve.wait_ge(ot_hi_ready, n * UNITS + (w + 1))
                dve.wait_ge(o_sum_done, n * UNITS * 2 + (2 * w + 2))
                nc.vector.tensor_tensor(ot_lo[block].rearrange("p t e q -> p t (e q)"),
                                        o_sum[:, :].rearrange("p (t q) -> p t q", q=P),
                                        f32(ot_hi[block].rearrange("p t e q -> p t (e q)")), ALU.subtract)\
                    .then_inc(ot_ready, 1)

            def group(n, b, g, m, last_x):
                for s in range(STEPS + 2):
                    for k in DVE_SPLIT:
                        if isinstance(m, int) and m == 0 and s == SPLIT_STEP[k]:
                            first_split_lo(k)
                    if n is not None and s < TASKS:
                        row_max(n, s)
                    if n is not None and 1 <= s <= TASKS:
                        normalise_p(n, s - 1)
                    if n is not None and 2 <= s < TASKS + 2:
                        pt_low(n, s - 2)
                    if n is not None and s >= 8 and s % 4 == 0:
                        o_add(n, (s - 8) // 4)
                    if n is not None and s >= 9 and s % 4 == 1:
                        ot_low(g, n, (s - 9) // 4)
                    if m is not None and s == 17:
                        v_low(m, 0)
                    if last_x and s in (17, 19):
                        x_round(b + 1, s - 17)
                        x_low(b + 1, s - 17)
                    if m is not None:
                        for u, j in ROUND_STEP.get(s - 1, []):
                            qk_low(m, u, j)
                    if m is not None and s == STEPS:
                        v_low(m, 1)

            def prologue():
                for x in range(X_UNITS):
                    if x % 2 == 0:
                        x_round(0, x)
                    x_low(0, x)
                group(None, 0, 0, 0, False)

            def body(b, g, ahead, fill=True, new_x=False, last_x=False):
                n = b * GROUPS + g
                group(n, b, g, n + 1 if fill else None, last_x)

            def tail(b, groups):
                def half_stats(t, h):
                    nc.vector.bn_stats(stats[:, t, 6 * h:6 * h + 6], y[t][:, h * HALF:(h + 1) * HALF])\
                        .then_inc(stats_done, 1)

                def row_stats(which, t, stats_seen):
                    dve.wait_ge(stats_done, b * 16 + stats_seen)
                    nc.vector.memset(turn[:, 2 + t:3 + t], 0.0).then_inc(mv_done, 1)
                    nc.vector.bn_aggr(mean_var[:, t, :], stats[:, t, :]).then_inc(mv_done, 1)
                    dve.wait_ge(mv_done, b * 16 + 2 * (4 * which + t + 1))
                    nc.vector.tensor_scalar(var_eps[:, t:t + 1], mean_var[:, t, 1:2], EPS, None, ALU.add)\
                        .then_inc(ve_done, 1)

                def normalise(which, t, ready):
                    dve.wait_ge(rstd_ready, b * 8 + (4 * which + t + 1))
                    nc.vector.tensor_scalar(y[t][:, :], y[t][:, :], mean_var[:, t, 0:1], rstd[:, t:t + 1],
                                            ALU.subtract, ALU.mult).then_inc(ready, 1)

                def x1t_low(t):
                    for k in range(2):
                        dve.wait_ge(x1t_hi_ready, b * 8 + (2 * t + k + 1))
                        nc.vector.tensor_tensor(ot_lo[:, t, 4 * k:4 * k + 4, :],
                                                u_ps[k][:, :].rearrange("p (e q) -> p e q", e=4),
                                                f32(ot_hi[:, t, 4 * k:4 * k + 4, :]), ALU.subtract)\
                            .then_inc(x1t_ready, 1)

                for q in range(2 * TOK_TILES):
                    h, t = q // TOK_TILES, q % TOK_TILES
                    if h == 0:
                        dve.wait_ge(y_loaded[t], b * 16 + 16)
                    cols = slice(h * HALF, (h + 1) * HALF)
                    dve.wait_ge(op_done, b * 8 + (q + 1))
                    nc.vector.tensor_tensor(y[t][:, cols], op_ps[h][t][:, :], y[t][:, cols], ALU.add)\
                        .then_inc(op_added, 1)
                    dve.wait_ge(op_added, b * 8 + (q + 1))
                    half_stats(t, h)
                    if h == 1:
                        row_stats(0, t, q + 1)
                        if t == 2:
                            x1t_low(0)
                        if t >= 1:
                            normalise(0, t - 1, x1_done)
                normalise(0, TOK_TILES - 1, x1_done)

                dve.wait_ge(scale_ready, 1)
                for t in range(TOK_TILES):
                    for h in range(2):
                        q = 2 * t + h + 1
                        cols = slice(h * HALF, (h + 1) * HALF)
                        dve.wait_ge(ffn_done, b * 8 + q)
                        nc.vector.tensor_tensor(z_mul_sb[h][:, :], t_ps[h][:, :], scale_sb[:, cols], ALU.mult)\
                            .then_inc(z_mul, 1)
                        dve.wait_ge(z_mul, b * 8 + q)
                        nc.vector.tensor_tensor(y[t][:, cols], z_mul_sb[h][:, :], y[t][:, cols], ALU.add)\
                            .then_inc(z_added, 1)
                        dve.wait_ge(z_added, b * 8 + q)
                        half_stats(t, h)
                        if h == 0 and t + 1 < TOK_TILES:
                            x1t_low(t + 1)
                    row_stats(1, t, 8 + 2 * t + 2)
                    if t >= 1:
                        normalise(1, t - 1, z_done)
                normalise(1, TOK_TILES - 1, z_done)

            program(body, tail, prologue, dve)

        @block.tensor
        def _(pe):
            def three(out_ap, a_hi, a_lo, b_hi, b_lo, first, last):
                nc.tensor.matmul(out_ap, a_hi, b_lo, start=first, stop=False)
                nc.tensor.matmul(out_ap, a_lo, b_hi, start=False, stop=False)
                return nc.tensor.matmul(out_ap, a_hi, b_hi, start=False, stop=last)

            def project_qk(m, tails, u, e, new_x_batch):
                if e == 0:
                    pe.wait_ge(w_ready, g_pos(m, tails) + (u + 1))
                    if u >= 2:
                        pe.wait_ge(qk_evacuated, m * QKU + (u - 1))
                    elif not (isinstance(m, int) and m == 0):
                        pe.wait_ge(v_ready, m * VU + (u - 1))
                if u == 0 and new_x_batch is not None and e % 2 == 0:
                    pe.wait_ge(x_ready[e // 2], new_x_batch + 1)
                slot = G_SLOT[u]
                cols = slice(e * P, (e + 1) * P)
                mm = three(u_ps[u % 2][:, :], w_hi[slot][:, cols], w_lo[slot][:, cols],
                           x_hi[:, e, :], x_lo[:, e, :], e == 0, e == E_TILES - 1)
                if e == E_TILES - 1:
                    mm.then_inc(qk_done, 1)

            def project_v(m, tails, v, half, e):
                t = (2 if v == 0 else 0) + half
                if e % 4 == 0 and half == 0 and v == 0:
                    pe.wait_ge(w_ready, g_pos(m, tails) + (5 + e // 4))
                if e == 0 and half == 0:
                    pe.wait_ge(qk_evacuated, m * QKU + (3 + v))
                width = GROUP_HEADS * HEAD_DIM
                slot, cols = 2 + e // 4, slice((e % 4) * width, (e % 4 + 1) * width)
                tok = slice(t * P, (t + 1) * P)
                mm = three(u_ps[v][:, half * width:(half + 1) * width], x_hi[:, e, tok], x_lo[:, e, tok],
                           w_hi[slot][:, cols], w_lo[slot][:, cols],
                           e == 0 and half == 0, e == E_TILES - 1 and half == 1)
                if half == 1 and e == E_TILES - 1:
                    mm.then_inc(v_done, 1)
                elif v == 1 and half == 1 and e % 2 == 1:
                    mm.then_inc(x_used, 1)

            def fill_pieces(m, tails, new_x_batch):
                pieces = []
                for u in range(QKU):
                    pieces += [(project_qk, (m, tails, u, e, new_x_batch)) for e in range(E_TILES)]
                for v in range(VU):
                    for e2 in range(2 * E_TILES):
                        pieces.append((project_v, (m, tails, v, e2 % 2, e2 // 2)))
                return pieces

            def piece_range(s):
                u, third = s // 3, s % 3
                if u < QKU:
                    cut = [0, 3, 6, 8]
                    return u * 8 + cut[third], u * 8 + cut[third + 1]
                first = 8 * QKU + 4 * (s - 3 * QKU)
                return first, first + 4

            def scores(n, tau):
                i, j, w = task(tau)
                if tau % 4 == 0 and tau < PAIRS:
                    pe.wait_ge(q_ready, n * GROUP_HEADS + (tau // 2 + 2))
                    pe.wait_ge(k_ready, n * GROUP_HEADS + (tau // 2 + 2))
                if tau >= 2:
                    pe.wait_ge(max_done, n * TASKS * 2 + 2 * (tau - 1))
                rows, tok, bank = head_rows(j % 2)[0], slice(i * P, (i + 1) * P), s_ps[tau % 2][:, 0:w]
                nc.tensor.matmul(bank, q_st[rows, j, tok], k_lo[rows, j // 2, 0:w], start=True, stop=False)
                nc.tensor.matmul(bank, q_st[:, j, tok], k_st[:, j, 0:w], start=False, stop=True)\
                    .then_inc(s_done, 1)

            def transpose_p(n, tau):
                i = task(tau)[0]
                if tau >= 2:
                    pe.wait_ge(pt_ready, n * TASKS + (tau - 1))
                pe.wait_ge(norm_done, n * TASKS + (tau + 1))
                for k in range(i + 1):
                    mm = nc.tensor.transpose(t_ps[tau % 2][:, k * P:(k + 1) * P],
                                             prob[tau % 3][:, k * P:(k + 1) * P], ident[:, :])
                mm.then_inc(t_done, 1)

            def weigh_values(n, p):
                i, j, _ = task(2 * p)
                w = p // 2
                if p == 0:
                    pe.wait_ge(v_ready, n * VU + VU)
                if w >= 2 and p % 2 == 0:
                    pe.wait_ge(o_sum_done, n * UNITS * 2 + 2 * (w - 1))
                pe.wait_ge(pt_ready, n * TASKS + (2 * p + 2))
                o = o_ps[w % 2][:, p % 2 * 2 * P:(p % 2 + 1) * 2 * P]
                for k in range(i + 1):
                    q = slice(0 if k < i else P, 2 * P)
                    nc.tensor.matmul(o[:, q], v_sb[:, k, j, :], pt_lo[p % 2][:, k, q], start=p % 2 == 0 and k == 0,
                                     stop=False)
                    mm = nc.tensor.matmul(o[:, q], v_sb[:, k, j, :], pt_hi[p % 2][:, k, q],
                                          start=False, stop=k == i and p % 2 == 1)
                mm.then_inc(pv_done, 1)

            def group(n, b, m, tails, new_x_batch):
                pieces = fill_pieces(m, tails, new_x_batch) if m is not None else []
                for s in range(STEPS):
                    late = s == 0 and n is not None and new_x_batch is None
                    if n is not None:
                        if s < TASKS and not late:
                            scores(n, s)
                        if 2 <= s < TASKS + 2:
                            transpose_p(n, s - 2)
                        if s >= 5 and s % 2 == 1:
                            weigh_values(n, (s - 5) // 2)
                    if m is not None:
                        first, end = piece_range(s)
                        for work, args in pieces[first:end]:
                            work(*args)
                    for i, at in enumerate(EARLY_STEP):
                        if m is None and at == s:
                            (u, t), part = EARLY_OUT[i // 2], i % 2
                            project_out(b, n + 1, u, t, t == 2 and part == 0, False, [part])
                    if late:
                        scores(n, s)

            def project_out(b, groups, u, t, first, last, parts=(0, 1)):
                h, w = u // 4, u % 4
                if first:
                    pe.wait_ge(w_ready, wo_pos(groups, b) + (u + 1))
                    if h == 0:
                        pe.wait_ge(ot_ready, b * 16 + 4 * (w + 1))
                if u == 0 and t >= 2 and 0 in parts:
                    pe.wait_ge(v_ready, groups * VU - (3 - t))
                for k in parts:
                    e, cols = 2 * w + k, slice(k * HALF, (k + 1) * HALF)
                    mm = three(op_ps[h][t][:, :], ot_hi[:, t, e, :], ot_lo[:, t, e, :],
                               w_hi[w][:, cols], w_lo[w][:, cols], e == 0, e == E_TILES - 1)
                if w == 3:
                    mm.then_inc(op_done, 1)
                elif last and u < 6:
                    mm.then_inc(wo_slot_free, 1)

            def prologue():
                pe.wait_ge(consts_ready, 1)
                group(None, 0, 0, 0, 0)

            def body(b, g, ahead, fill=True, new_x=False, last_x=False):
                n = b * GROUPS + g
                group(n, b, n + 1 if fill else None, b, b + 1 if new_x else None)

            def tail(b, groups):
                def transpose_x1(t):
                    pe.wait_ge(x1_done, b * TOK_TILES + (t + 1))
                    for e in range(E_TILES):
                        mm = nc.tensor.transpose(u_ps[e // 4][:, (e % 4) * P:(e % 4 + 1) * P],
                                                 y[t][:, e * P:(e + 1) * P], ident[:, :])
                        if e % 4 == 3:
                            mm.then_inc(x1tt_done, 1)

                for u in range(6):
                    tiles = [t for t in range(TOK_TILES) if groups is not BATCHES * GROUPS or (u, t) not in EARLY_OUT]
                    for t in tiles:
                        project_out(b, groups, u, t, t == 0, t == tiles[-1])
                for t in range(TOK_TILES):
                    if t == TOK_TILES - 1:
                        transpose_x1(0)
                    for u in (6, 7):
                        project_out(b, groups, u, t, t == 0, False)

                for t in range(TOK_TILES):
                    pe.wait_ge(x1t_ready, b * 8 + (2 * t + 2))
                    for h in range(2):
                        if t >= 1:
                            pe.wait_ge(z_mul, b * 8 + (2 * t + h - 1))
                        for e in range(E_TILES):
                            f = 4 * h + e // 2
                            if t == 0 and e % 2 == 0:
                                pe.wait_ge(w8_ready, b * 8 + (W8_ORDER.index(f) + 1))
                            slot = w_hi[f] if f < 4 else w_lo[f - 4]
                            cols = slice((e % 2) * HALF, (e % 2 + 1) * HALF)
                            nc.tensor.matmul(t_ps[h][:, :], ot_lo[:, t, e, :], slot[:, cols],
                                             start=e == 0, stop=False)
                            mm = nc.tensor.matmul(t_ps[h][:, :], ot_hi[:, t, e, :], slot[:, cols],
                                                  start=False, stop=e == E_TILES - 1)
                            if t == TOK_TILES - 1 and h == 1 and e in (1, 3, 5):
                                mm.then_inc(w8_free, 1)
                        mm.then_inc(ffn_done, 1)
                        if h == 0 and t + 1 < TOK_TILES:
                            transpose_x1(t + 1)

            program(body, tail, prologue, pe)


def kernel(**inputs):
    import numpy as np
    import concourse.bacc as bacc
    from concourse.bass_utils import run_bass_kernel_spmd

    x = np.asarray(inputs["L0_attn_hidden_states"])
    wq, wk, wv, wo = (np.asarray(inputs[f"L0_attn_w_{s}"]) for s in ("q", "k", "v", "out"))
    w8 = np.asarray(inputs["L0_ffn_weight"])
    scales = np.asarray(inputs["L0_ffn_scales"])

    x_units = x.transpose(0, 2, 1).reshape(BATCHES, X_UNITS, 2, P, SEQ).transpose(0, 1, 3, 2, 4)
    x_units = x_units.reshape(BATCHES * X_UNITS, P, UNIT)

    def qk_unit(w, g, pair):
        rows = w[(GROUP_HEADS * g + 2 * pair) * HEAD_DIM:][:2 * HEAD_DIM]
        rows = rows.reshape(2, HEAD_DIM // 2, 2, EMBED).transpose(0, 2, 1, 3).reshape(P, E_TILES, P)
        return rows.transpose(2, 1, 0).reshape(P, UNIT)

    def v_unit(g, half):
        width = GROUP_HEADS * HEAD_DIM
        rows = wv[g * width:(g + 1) * width].reshape(width, E_TILES, P)[:, 4 * half:4 * half + 4]
        return rows.transpose(2, 1, 0).reshape(P, UNIT)

    def out_unit(w, u):
        h, e = u // 4, 2 * (u % 4)
        rows = w[h * HALF:(h + 1) * HALF].reshape(HALF, E_TILES, P)[:, e:e + 2]
        return rows.transpose(2, 1, 0).reshape(P, UNIT)

    units = []
    for g in [1, 2, 3, 0]:
        units += [qk_unit(wq, g, 0), qk_unit(wk, g, 0), qk_unit(wq, g, 1), qk_unit(wk, g, 1)]
        units += [v_unit(g, 0), v_unit(g, 1)]
    units += [out_unit(wo, u) for u in range(WO_UNITS)]
    w_units = np.stack(units)
    w8_units = np.stack([out_unit(w8, u) for u in range(W8_UNITS)]).reshape(W8_UNITS // 2, 2, P, UNIT)
    w8_units = w8_units.transpose(0, 2, 1, 3).reshape(W8_UNITS // 2, P, 2 * UNIT)
    w8_units = np.ascontiguousarray(w8_units).view(np.int32)

    freq = (np.float32(1.0) / np.float32(10000.0) ** (np.arange(0, HEAD_DIM, 2, dtype=np.float32)
                                                       / np.float32(HEAD_DIM))).astype(np.float32)
    angle = (np.arange(SEQ, dtype=np.float32)[None, :] * freq[:, None]).astype(np.float32)
    cos32, sin32 = np.cos(angle), np.sin(angle)
    cos_table = np.concatenate([cos32, cos32, cos32, cos32])
    sin_table = np.concatenate([-sin32, sin32, -sin32, sin32])

    arrays = {
        "x_units": x_units, "x_rows": x.reshape(BATCHES * TOK_TILES, P, EMBED), "w_units": w_units,
        "w8_units": w8_units, "scales": scales.reshape(EMBED), "cos_table": cos_table, "sin_table": sin_table,
    }
    arrays = {k: np.ascontiguousarray(v) for k, v in arrays.items()}
    nc = bacc.Bacc("TRN2", target_bir_lowering=False, num_devices=1)
    args = [nc.dram_tensor(k, v.shape, mybir.dt.from_np(v.dtype), kind="ExternalInput").ap()
            for k, v in arrays.items()]
    out = nc.dram_tensor("out", (BATCHES * TOK_TILES, P, EMBED), F32, kind="ExternalOutput").ap()
    layer_program(nc, *args, out)
    result = run_bass_kernel_spmd(nc, [arrays], core_ids=[0])
    return result.results[0]["out"].reshape(BATCHES, SEQ, EMBED)
```
